# Optimizing a Trainium2 kernel written in Bass

```python
import numpy as np
import jax
import jax.numpy as jnp

def _softmax(x, axis=-1):
    return jax.nn.softmax(x, axis=axis)

def _gelu(x):
    return jax.nn.gelu(x, approximate=True)

def _silu(x):
    return jax.nn.silu(x)

def _sigmoid(x):
    return jax.nn.sigmoid(x)

def _layernorm(x, axis=-1, eps=1e-05):
    m = jnp.mean(x, axis=axis, keepdims=True)
    v = jnp.var(x, axis=axis, keepdims=True)
    return (x - m) / jnp.sqrt(v + eps)

def _scatter_add(tgt, idx, src, axis=0):
    return tgt.at[idx].add(src)

def _segment_sum(src, seg, n):
    return jax.ops.segment_sum(src, seg, n)
kernel_name = 'mk_gnn_resnorm_d2_gnn_r32_08b7fe'

def setup_inputs(seed: int=0):
    np.random.seed(seed)
    _w = jnp.asarray

    def _rec_inputs():
        import jax
        import jax.numpy as jnp
        _gk = jax.random.key(seed)
        x = -0.0002117 + 1 * jax.random.normal(jax.random.fold_in(_gk, 1), (3125, 256), jnp.float32)
        src = jax.random.randint(jax.random.fold_in(_gk, 2), (50000,), 0, 3125, jnp.int32)
        dst = jnp.minimum((3125 * jax.random.uniform(jax.random.fold_in(_gk, 3), (50000,)) ** 2.0).astype(jnp.int32), 99999)
        _o = jnp.argsort(dst, stable=True)
        src = src[_o]
        dst = dst[_o]
        edge_weight = jax.random.uniform(jax.random.fold_in(_gk, 12), (50000,), jnp.float32, 0.0, 1)
        return (x, src, dst, edge_weight)
    x, src, dst, edge_weight = _rec_inputs()

    def _L0_gnn_setup():
        import jax, jax.numpy as jnp
        import numpy as np
        N_NODES = 3125
        N_EDGES = 50000
        IN_FEATS = 256
        OUT_FEATS = 256
        key = jax.random.key(seed)
        k_h, k_norm, k_w, k_b, k_src, k_dst = jax.random.split(key, 6)
        stdv = 1.0 / np.sqrt(OUT_FEATS)
        return {'h': jax.random.normal(k_h, (N_NODES, IN_FEATS), dtype=jnp.float32), 'sym_norm': jax.random.uniform(k_norm, (N_EDGES,), dtype=jnp.float32), 'W': jax.random.uniform(k_w, (IN_FEATS, OUT_FEATS), dtype=jnp.float32, minval=-stdv, maxval=stdv), 'b': jax.random.uniform(k_b, (OUT_FEATS,), dtype=jnp.float32, minval=-stdv, maxval=stdv), 'src': jax.random.randint(k_src, (N_EDGES,), 0, N_NODES, dtype=jnp.int32), 'dst': jax.random.randint(k_dst, (N_EDGES,), 0, N_NODES, dtype=jnp.int32)}
    _L0_gnn_all = _L0_gnn_setup()
    _L0_gnn_in = {k: v for k, v in _L0_gnn_all.items() if k in ('W', 'b')}
    del _L0_gnn_all

    def _L1_gnn_setup():
        import jax, jax.numpy as jnp
        import numpy as np
        N_NODES = 50000
        N_EDGES = 25000
        HIDDEN = 256
        K_HOP = 3
        key = jax.random.key(seed)
        k1, k2, k3, k4 = jax.random.split(key, 4)
        x = jax.random.normal(k1, (N_NODES, HIDDEN), dtype=jnp.float32)
        W = jax.random.normal(k2, (K_HOP, HIDDEN, HIDDEN), dtype=jnp.float32) / jnp.sqrt(HIDDEN).astype(jnp.float32)
        b = jnp.zeros((K_HOP, HIDDEN), dtype=jnp.float32)
        src = jax.random.randint(k3, (N_EDGES,), 0, N_NODES, dtype=jnp.int32)
        dst = jax.random.randint(k4, (N_EDGES,), 0, N_NODES, dtype=jnp.int32)
        return {'x': x, 'W': W, 'b': b, 'src': src, 'dst': dst}
    _L1_gnn_all = _L1_gnn_setup()
    _L1_gnn_in = {k: v for k, v in _L1_gnn_all.items() if k in ('W', 'b')}
    del _L1_gnn_all
    return {'x': x, 'src': src, 'dst': dst, 'edge_weight': edge_weight, 'L0_gnn_W': _L0_gnn_in['W'], 'L0_gnn_b': _L0_gnn_in['b'], 'L1_gnn_W': _L1_gnn_in['W'], 'L1_gnn_b': _L1_gnn_in['b']}

def reference(x, src, dst, edge_weight, L0_gnn_W, L0_gnn_b, L1_gnn_W, L1_gnn_b):
    import jax
    import jax.numpy as jnp

    def _L0_gnn_ref(h, sym_norm, W, b, src, dst):
        import jax, jax.numpy as jnp
        import numpy as np
        N_NODES = 3125
        N_EDGES = 50000
        IN_FEATS = 256
        OUT_FEATS = 256
        n_nodes = h.shape[0]
        hw = jnp.matmul(h, W)
        msg = hw[src] * sym_norm[:, None]
        agg = jax.ops.segment_sum(msg, dst, num_segments=n_nodes)
        return jax.nn.relu(agg + b)

    def _L1_gnn_ref(x, W, b, src, dst):
        import jax, jax.numpy as jnp
        import numpy as np
        N_NODES = 50000
        N_EDGES = 25000
        HIDDEN = 256
        K_HOP = 3
        N = x.shape[0]
        ones = jnp.ones(src.shape[0], dtype=x.dtype)
        out_deg = jax.ops.segment_sum(ones, src, num_segments=N)
        in_deg = jax.ops.segment_sum(ones, dst, num_segments=N)
        out_norm = jnp.clip(out_deg, 1.0, None) ** (-0.5)
        in_norm = jnp.clip(in_deg, 1.0, None) ** (-0.5)
        k_hop = W.shape[0]
        h = x
        for i in range(k_hop):
            h = h * out_norm[:, None]
            h = jax.ops.segment_sum(h[src], dst, num_segments=N)
            h = h * in_norm[:, None]
            h = h @ W[i] + b[i]
            if i < k_hop - 1:
                h = jax.nn.relu(h)
        return h
    x = _layernorm(x + _L0_gnn_ref(x, edge_weight, L0_gnn_W, L0_gnn_b, src, dst), axis=-1)
    x = _layernorm(x + _L1_gnn_ref(x, L1_gnn_W, L1_gnn_b, src, dst), axis=-1)
    return x

_drawn_inputs = setup_inputs


def setup_inputs(seed=0):
    import zlib

    import numpy as np

    out = dict(_drawn_inputs(seed))
    spreads = {'L1_gnn_b': (0.0, 0.1)}
    factors = {'L0_gnn_b': 2.893}
    for name, (base, spread) in spreads.items():
        noise = np.random.default_rng([zlib.crc32(name.encode()), seed]).standard_normal(out[name].shape)
        drawn = base * np.exp(spread * noise) if base else spread * noise
        out[name] = jnp.asarray(drawn.astype(out[name].dtype))
    for name, factor in factors.items():
        out[name] = (out[name] * factor).astype(out[name].dtype)
    return out
```

```python
import concourse.bass as bass
from concourse import mybir
from contextlib import ExitStack

F32 = mybir.dt.float32
F16 = mybir.dt.float16
BF16 = mybir.dt.bfloat16
I32 = mybir.dt.int32
ALU = mybir.AluOpType
ACT = mybir.ActivationFunctionType
AX = mybir.AxisListType

P = 128
N, D, E = 3125, 256, 50000
HOPS = 3
NT = -(-N // P)
NLAST = N - (NT - 1) * P
NPAD = NT * P
HALVES = D // P
PARTS = 3
BC = 2
UB = 4
UC = UB * BC
NU = -(-E // (P * UC))
CH = NU * UC
NB = NU * UB
W = 64
WA = 32
ND = 1536
GC = 512
GD = ND // GC
AW = ND + WA
ACCW = NPAD + W
MN = NT * WA
QSTEP = 5
STEPS = NT // QSTEP
PAD_DST = 8000
EXACT = 256.0
EPS = 1e-5


def gnn_program(nc, x, src_c, dst_c, wt_c, dst_r, w0, b0, w1, b1, out):
    ctx = ExitStack()
    with ctx:
        def sb(name, shape, dt):
            return ctx.enter_context(nc.sbuf_tensor(name, shape, dt))

        def ps(name, shape):
            return ctx.enter_context(nc.psum_tensor(name, shape, F32))

        def sem(name):
            return ctx.enter_context(nc.semaphore(name))

        stat_d = nc.dram_tensor("stat_d", (2, NB), F32).ap()
        x1_d = nc.dram_tensor("x1_d", (NPAD, D), F32).ap()
        hp_d = nc.dram_tensor("hp_d", (N, PARTS * D), BF16).ap()

        src = sb("src", [P, CH], I32)
        dst_i = sb("dst_i", [P, CH], I32)
        wt = sb("wt", [P, CH], F32)
        dst = sb("dst", [P, CH], F32)
        dloc = sb("dloc", [P, CH], F32)
        dsel = sb("dsel", [P, CH], F32)
        key = sb("key", [P, CH], F32)
        tmp = sb("tmp", [P, CH], F32)
        srcq = sb("srcq", [P, CH], F32)
        srcq_h = sb("srcq_h", [P, CH], BF16)
        srcr_h = sb("srcr_h", [P, CH], BF16)
        dstq_h = sb("dstq_h", [P, CH], BF16)
        dstr_h = sb("dstr_h", [P, CH], BF16)
        srow = sb("srow", [NB // BC, 2, BC], F32)
        stat = sb("stat", [P, 2, NB], F32)
        gbase = sb("gbase", [P, NB], F32)
        abase = sb("abase", [P, NB], F32)
        gtab = sb("gtab", [P, BC + NB], I32)
        atab = sb("atab", [P, BC + NB], I32)
        bt0 = sb("bt0", [P, NB], F32)
        bt1 = sb("bt1", [P, NB], F32)
        bi0 = sb("bi0", [P, NB], I32)
        bi1 = sb("bi1", [P, NB], I32)
        uidx = sb("uidx", [P, NB], F32)
        scf = sb("scf", [P, 4], F32)
        scal = sb("scal", [P, 4], I32)
        thr = sb("thr", [P, 2], F32)
        iotm = sb("iotm", [P, MN], F16)
        iotr = sb("iotr", [P, P], BF16)
        iotw = sb("iotw", [P, W], F32)
        zeros = sb("zeros", [P, GC], BF16)
        ones = sb("ones", [P, P], F32)
        zcol = sb("zcol", [P, 1], F32)
        epsc = sb("epsc", [P, 1], F32)
        W0 = sb("W0", [P, HALVES, D], F32)
        W1 = sb("W1", [P, HOPS, HALVES, D], F32)
        b0s = sb("b0s", [1, D], F32)
        b1s = sb("b1s", [P, HOPS, D], F32)
        A = sb("A", [P, NT, AW], BF16)
        hp = sb("hp", [P, NT, PARTS, D], BF16)
        acc = sb("acc", [P, HALVES, ACCW], F32)
        rows = sb("rows", [P, UC, PARTS * D], BF16)
        rows_f = rows[:, :, :].bitcast(F32)
        stage = sb("stage", [P, UC], I32)
        hot_1 = sb("hot_1", [P, UC, W], BF16)
        hp_flat = hp[:, :, :, :].rearrange("p q k d -> p (q k d)")
        at_r = UC * MN
        at_q = at_r + 2 * UC * P
        at_w = at_q + 2 * UC * NT
        hot_m = hp_flat[:, 0:at_r].rearrange("p (k m) -> p k m", k=UC)
        hot_r = hp_flat[:, at_r:at_q].rearrange("p (h k m) -> p h k m", h=2, k=UC)
        hot_q = hp_flat[:, at_q:at_w].rearrange("p (h k m) -> p h k m", h=2, k=UC)
        hot_w = hp_flat[:, at_w:at_w + 2 * UC * W].bitcast(F32).rearrange("p (k m) -> p k m", k=UC)
        at_t = at_w + 2 * UC * W
        itmp = hp_flat[:, at_t:at_t + 2 * CH].bitcast(I32)
        at_d = at_t + 2 * CH
        RD = BC * BC * P
        drow_i = hp_flat[0:NB // BC, at_d:at_d + 2 * RD].bitcast(I32)
        drow = hp_flat[0:NB // BC, at_d + 2 * RD:at_d + 4 * RD].bitcast(F32)
        norm = sb("norm", [P, 2, NT], F32)
        viol = sb("viol", [P, 1], F32)
        xin = sb("xin", [P, 4, D], F32)
        xp = sb("xp", [P, 4, D], F32)
        vv = sb("vv", [P, 4, D], F32)
        bst = sb("bst", [P, 4, 6], F32)
        mv = sb("mv", [P, 4, 2], F32)
        sd = sb("sd", [P, 4], F32)
        rs = sb("rs", [P, 4], F32)

        psA = [ps(f"psA{i}", [P, 2 * GC]) for i in range(2)]
        psG = ps("psG", [P, GC])
        psH = ps("psH", [P, GC])
        psW = [ps(f"psW{i}", [P, GC]) for i in range(2)]
        hist = psH[:, 0:2 * NT].rearrange("p (k q) -> p k q", k=2)


        def shares(f):
            return [bank[:, 0:HALVES * W].rearrange("p (h d) -> p h d", h=HALVES)
                    for bank in (psG, psH if f else psW[1])]

        s_in = sem("s_in")
        s_inr = sem("s_inr")
        s_wts = sem("s_wts")
        s_iota = sem("s_iota")
        s_const = sem("s_const")
        s_hist = sem("s_hist")
        s_srow = sem("s_srow")
        s_sd = sem("s_sd")
        s_st = sem("s_st")
        s_scal = sem("s_scal")
        s_dve = sem("s_dve")
        s_tick = sem("s_tick")
        s_viol = sem("s_viol")
        s_vsum = sem("s_vsum")
        s_deg = sem("s_deg")
        s_norm = sem("s_norm")
        s_bld = sem("s_bld")
        s_adda = sem("s_adda")

        def phase_sems(name):
            return {
                "landed": [sem(f"{name}_landed{k}") for k in range(UC)],
                "staged": sem(f"{name}_staged"),
                "hot": sem(f"{name}_hot"),
                "done": sem(f"{name}_done"),
                "added": sem(f"{name}_added"),
                "round": sem(f"{name}_round"),
                "dense": sem(f"{name}_dense"),
                "aggr": sem(f"{name}_aggr"),
                "lin": sem(f"{name}_lin"),
                "xin": [sem(f"{name}_xin{k}") for k in range(4)],
                "free": sem(f"{name}_free"),
                "var": sem(f"{name}_var"),
                "std": sem(f"{name}_std"),
                "nrm": sem(f"{name}_nrm"),
                "vhi": sem(f"{name}_vhi"),
                "rem": sem(f"{name}_rem"),
                "mid": sem(f"{name}_mid"),
                "low": sem(f"{name}_low"),
                "out": [sem(f"{name}_out{k}") for k in range(4)],
                "hpd": sem(f"{name}_hpd"),
            }

        S = [phase_sems(f"f{k}") for k in range(HOPS + 1)]

        def tile_rows(t):
            return P if t < NT - 1 else NLAST

        def rounds_of(eng):
            return eng.value_load(scal[0:1, 0:1], min_val=1, max_val=NPAD // WA + 1)

        def build_units_of(eng):
            return eng.value_load(scal[0:1, 1:2], min_val=1, max_val=NU)

        def first_unit_of(eng):
            return eng.value_load(scal[0:1, 2:3], min_val=0, max_val=NU - 1)

        def hop_units_of(eng):
            return eng.value_load(scal[0:1, 3:4], min_val=1, max_val=NU)

        def first_block_loops(eng, unit, ahead=None, after_build=None, after=None):
            eng.wait_ge(s_scal, 1)
            rounds = rounds_of(eng)
            nbu = build_units_of(eng)
            with eng.Fori(0, rounds) as j:
                if ahead:
                    ahead(j)
                with eng.Fori(0, nbu) as u:
                    unit(u, j * NU + u, j * nbu + u, j, nbu)
                if after_build:
                    after_build(j * nbu + nbu, j, nbu)
                with eng.If(nbu < NU):
                    with eng.Fori(nbu, NU) as u:
                        unit(u, j * NU + u, None, j, nbu)
                if after:
                    after(j * NU + NU, j)

        def hop_loops(eng, unit, ahead=None, after=None):
            rounds = rounds_of(eng)
            first = first_unit_of(eng)
            units = hop_units_of(eng)
            with eng.Fori(0, rounds) as j:
                if ahead:
                    ahead(j)
                with eng.Fori(0, units) as i:
                    u = nc.s_assert_within(first + i, 0, NU - 1, skip_runtime_bounds_check_because="first + units = NU")
                    unit(u, j * units + i, j)
                if after:
                    after((j + 1) * units, j)
            return rounds * (units * UB + BC) + 1

        def psD(g, h):
            return psA[g][:, h * GC:(h + 1) * GC] if g < 2 else psW[h][:, :]

        block = ctx.enter_context(nc.Block())

        @block.sync
        def _(sp):
            sp.dma_start(drow_i[:, :], dst_r).then_inc(s_inr, 16)
            sp.dma_start(src[:, :], src_c).then_inc(s_in, 16)
            sp.dma_start(dst_i[:, :], dst_c).then_inc(s_in, 16)
            sp.dma_start(wt[:, :], wt_c).then_inc(s_in, 16)
            sp.wait_ge(s_srow, 1)
            sp.dma_start(stat_d.rearrange("k (p j) -> p k j", j=BC), srow[:, :, :]).then_inc(s_sd, 16)
            sp.wait_ge(s_sd, 16)
            sp.dma_start(stat[:, :, :], stat_d.unsqueeze(0).to_broadcast([P, 2, NB])).then_inc(s_st, 16)
            sp.dma_start(W0[:, :, :], w0.rearrange("(h p) n -> p h n", p=P)).then_inc(s_wts, 16)
            sp.dma_start(W1[:, :, :, :], w1.rearrange("k (h p) n -> p k h n", p=P)).then_inc(s_wts, 16)
            sp.dma_start(b0s[:, :], b0.unsqueeze(0)).then_inc(s_wts, 16)
            sp.dma_start(b1s[:, :, :], b1.unsqueeze(0).to_broadcast([P, HOPS, D])).then_inc(s_wts, 16)

            for f in range(HOPS + 1):
                s = S[f]
                last = f == HOPS
                source = x if f == 0 else x1_d

                def load(t):
                    k, n = t % 4, tile_rows(t)
                    if t >= 4:
                        sp.wait_ge(s["free"], t - 3)
                    if t == NT - 1 and f == 0:
                        sp.wait_ge(s_const, 2)
                    sp.dma_start(xin[0:n, k, :], source[t * P:t * P + n, :]).then_inc(s["xin"][k], 16)

                if f == 0 or last:
                    for t in range(3):
                        load(t)
                for t in range(NT):
                    n = tile_rows(t)
                    if f == 0 or last:
                        if t + 3 < NT:
                            load(t + 3)
                        sp.wait_ge(s["nrm"], t + 1)
                        to = x1_d[t * P:t * P + n, :] if f == 0 else out[t * P:t * P + n, :]
                        sp.dma_start(to, xp[0:n, t % 4, :]).then_inc(s["out"][t % 4], 16)
                    if not last:
                        sp.wait_ge(s["low"], t + 1)
                        sp.dma_start(hp_d[t * P:t * P + n, :],
                                     hp[0:n, t, :, :].rearrange("p k d -> p (k d)")).then_inc(s["hpd"], 16)
                if f == 0 or last:
                    for k in range(4):
                        sp.wait_ge(s["out"][k], 16 * len(range(k, NT, 4)))
                if not last:
                    sp.wait_ge(s["hpd"], 16 * NT)

        @block.gpsimd
        def _(pool):
            pool.iota(iotm[:, :], [[1, MN]], base=0, channel_multiplier=0,
                      allow_small_or_imprecise_dtypes=True).then_inc(s_iota, 1)
            pool.iota(iotr[:, :], [[1, P]], base=0, channel_multiplier=0,
                      allow_small_or_imprecise_dtypes=True).then_inc(s_iota, 1)
            pool.iota(iotw[:, :], [[1, W]], base=0, channel_multiplier=0,
                      allow_small_or_imprecise_dtypes=True).then_inc(s_iota, 1)
            pool.iota(uidx[:, :], [[1, NU], [0, UB]], base=0, channel_multiplier=0,
                      allow_small_or_imprecise_dtypes=True).then_inc(s_iota, 1)
            pool.memset(acc[:, :, :], 0.0).then_inc(S[0]["added"], 1)

            def gather_block(s, q, b, table, buf):
                pool.wait_ge(s["staged"], q * UB + b + 1)
                pool.sem_inc(s_tick, 1)
                for c in range(BC):
                    k = b * BC + c
                    pool.indirect_dma_start(buf(k), None, table,
                                            bass.IndirectOffsetOnAxis(ap=stage[:, k:k + 1], axis=0)
                                            ).then_inc(s["landed"][k], 16)

            def first_unit(u, q, qb, j, nbu):
                for b in range(UB):
                    gather_block(S[0], q, b, x, lambda k: rows_f[:, k, 0:D])

            first_block_loops(pool, first_unit)

            for f in range(1, HOPS + 1):
                s = S[f]
                pool.wait_ge(S[f - 1]["lin"], NT)
                pool.memset(acc[:, :, :], 0.0).then_inc(s["added"], 1)
                pool.wait_ge(S[f - 1]["hpd"], 16 * NT)
                pool.wait_ge(s_scal, 2)

                def hop_unit(u, q, j):
                    for b in range(UB):
                        gather_block(s, q, b, hp_d, lambda k: rows[:, k, :])

                hop_loops(pool, hop_unit)

        @block.scalar
        def _(act):
            act.wait_ge(s_const, 1)
            nc.scalar.copy(A[:, :, :].rearrange("p q d -> p (q d)").bitcast(F32),
                           zcol[:, 0:1].to_broadcast([P, NT * AW // 2])).then_inc(s_adda, 1)
            act.wait_ge(s_in, 48)

            def stage_unit(s, u, q):
                for b in range(UB):
                    act.wait_ge(s["done"], q * UB + b + 1)
                    nc.scalar.copy(stage[:, b * BC:(b + 1) * BC],
                                   src[:, bass.ds(u * UC + b * BC, BC)]).then_inc(s["staged"], 1)

            first_block_loops(act, lambda u, q, qb, j, nbu: stage_unit(S[0], u, q))

            act.wait_ge(s_deg, 1)
            nc.scalar.activation(norm[:, :, :], norm[:, :, :], ACT.Sqrt).then_inc(s_norm, 1)
            act.wait_ge(s_norm, 1)

            for f in range(HOPS + 1):
                s = S[f]
                last = f == HOPS
                if f > 0:
                    act.wait_ge(s_scal, 2)
                    hop_loops(act, lambda u, q, j: stage_unit(s, u, q))
                for t in range(NT + 2):
                    if (f == 0 or last) and t < NT:
                        act.wait_ge(s["var"], t + 1)
                        nc.scalar.activation(sd[:, t % 4:t % 4 + 1], mv[:, t % 4, 1:2], ACT.Sqrt,
                                             bias=epsc[:, 0:1]).then_inc(s["std"], 1)
                    a = t - 1
                    if not last and 0 <= a < NT:
                        act.wait_ge(s["nrm"], a + 1)
                        if a >= 4:
                            act.wait_ge(s["low"], a - 3)
                        scale = norm[:, 0, a:a + 1]
                        nc.scalar.activation(vv[:, a % 4, :], xp[:, a % 4, :], ACT.Relu if f else ACT.Copy,
                                             scale=scale)
                        nc.scalar.activation(hp[:, a, 0, :], xp[:, a % 4, :], ACT.Relu if f else ACT.Copy,
                                             scale=scale).then_inc(s["vhi"], 1)
                    m = t - 2
                    if not last and 0 <= m < NT:
                        act.wait_ge(s["rem"], m + 1)
                        nc.scalar.copy(hp[:, m, 1, :], vv[:, m % 4, :]).then_inc(s["mid"], 1)

        @block.vector
        def _(dve):
            chain = [0]

            def link(ins):
                chain[0] += 1
                ins.then_inc(s_dve, 1)
                dve.wait_ge(s_dve, chain[0])

            ops = {"ts": nc.vector.tensor_scalar, "tt": nc.vector.tensor_tensor,
                   "stt": nc.vector.scalar_tensor_tensor, "cp": nc.vector.tensor_copy,
                   "red": nc.vector.tensor_reduce, "set": nc.vector.memset,
                   "rec": nc.vector.reciprocal}

            def v(name, *args, **kw):
                link(ops[name](*args, **kw))

            nc.vector.memset(zcol[:, :], 0.0).then_inc(s_const, 1)
            v("set", zeros[:, :], 0.0)
            v("set", ones[:, :], 1.0)
            v("set", epsc[:, :], EPS)
            v("set", gtab[:, 0:BC], 0)
            v("set", atab[:, 0:BC], 0)
            nc.vector.memset(xin[:, :, :], 0.0).then_inc(s_const, 1)
            dve.wait_ge(s_inr, 16)
            v("cp", drow[:, :], drow_i[:, :])
            rows_v = drow[:, :].rearrange("p (j e) -> p j e", j=BC)
            v("red", srow[:, 0, :], rows_v, axis=AX.X, op=ALU.min)
            v("stt", drow[:, :], drow[:, :], float(NPAD), drow[:, :], ALU.is_lt, ALU.mult)
            nc.vector.tensor_reduce(srow[:, 1, :], rows_v, axis=AX.X, op=ALU.max).then_inc(s_srow, 1)
            dve.wait_ge(s_in, 48)
            v("cp", dst[:, :], dst_i[:, :])
            v("ts", itmp[:, :], dst_i[:, :], 7, None, ALU.arith_shift_right)
            v("cp", dstq_h[:, :], itmp[:, :])
            v("ts", itmp[:, :], dst_i[:, :], P - 1, None, ALU.bitwise_and)
            v("cp", dstr_h[:, :], itmp[:, :])
            v("ts", itmp[:, :], src[:, :], P - 1, None, ALU.bitwise_and)
            v("cp", srcr_h[:, :], itmp[:, :])
            v("ts", itmp[:, :], src[:, :], 7, None, ALU.arith_shift_right)
            v("cp", srcq[:, :], itmp[:, :])
            v("ts", tmp[:, :], dst[:, :], float(NPAD), 64.0, ALU.is_ge, ALU.mult)
            v("tt", srcq_h[:, :], srcq[:, :], tmp[:, :], ALU.add)

            dve.wait_ge(s_st, 16)
            dve.wait_ge(s_iota, 4)
            v("cp", gbase[:, :], stat[:, 0, :])
            v("ts", abase[:, :], stat[:, 0, :], float(ND), None, ALU.min)
            v("tt", bt0[:, :], stat[:, 1, :], stat[:, 0, :], ALU.subtract)
            v("cp", bi0[:, :], bt0[:, :])
            v("ts", bi0[:, :], bi0[:, :], W.bit_length() - 1, None, ALU.arith_shift_right)
            v("ts", bt1[:, :], stat[:, 1, :], float(ND - 1), None, ALU.min)
            v("tt", bt1[:, :], bt1[:, :], stat[:, 0, :], ALU.subtract)
            v("cp", bi1[:, :], bt1[:, :])
            v("ts", bi1[:, :], bi1[:, :], WA.bit_length() - 1, None, ALU.arith_shift_right)
            v("tt", bt0[:, :], bi0[:, :], bi1[:, :], ALU.max)
            v("red", scf[:, 0:1], bt0[:, :], axis=AX.X, op=ALU.max)
            v("ts", scf[:, 0:1], scf[:, 0:1], 1.0, 1.0, ALU.add, ALU.max)
            v("ts", bt0[:, :], uidx[:, :], 1.0, None, ALU.add)
            v("stt", bt1[:, :], stat[:, 0, :], float(ND), bt0[:, :], ALU.is_lt, ALU.mult)
            v("red", scf[:, 1:2], bt1[:, :], axis=AX.X, op=ALU.max)
            v("ts", scf[:, 1:2], scf[:, 1:2], 1.0, None, ALU.max)
            nc.vector.tensor_copy(scal[:, 0:2], scf[:, 0:2]).then_inc(s_scal, 1)

            def per_chunk(tab):
                return tab[:, :].unsqueeze(2).to_broadcast([P, NB, BC])

            def per_block(tab):
                return tab[:, :].rearrange("p (b c) -> p b c", c=BC)

            def run_chain(chained, done, steps):
                for i, make in enumerate(steps):
                    make().then_inc(chained, 1)
                    dve.wait_ge(chained, done + i + 1)
                dve.sem_inc(s_tick, 1)

            vec = nc.vector
            open_gather = [
                lambda: vec.tensor_tensor(per_block(dloc), per_block(dst), per_chunk(gbase), ALU.subtract),
                lambda: vec.tensor_copy(gtab[:, BC:], gbase[:, :]),
                lambda: vec.memset(shares(0)[0], 0.0),
                lambda: vec.memset(shares(0)[1], 0.0),
            ]
            open_build = [
                lambda: vec.tensor_tensor(per_block(key), per_block(dst), per_chunk(abase), ALU.subtract),
                lambda: vec.tensor_scalar(tmp[:, :], key[:, :], 0.0, None, ALU.is_ge),
                lambda: vec.scalar_tensor_tensor(tmp[:, :], key[:, :], float(WA), tmp[:, :], ALU.is_lt, ALU.mult),
                lambda: vec.scalar_tensor_tensor(tmp[:, :], dst[:, :], float(ND), tmp[:, :], ALU.is_lt, ALU.mult),
                lambda: vec.scalar_tensor_tensor(key[:, :], srcq[:, :], float(WA), key[:, :], ALU.mult, ALU.add),
                lambda: vec.scalar_tensor_tensor(key[:, :], key[:, :], 1.0, tmp[:, :], ALU.add, ALU.mult),
                lambda: vec.tensor_scalar(key[:, :], key[:, :], -1.0, None, ALU.add),
                lambda: vec.tensor_copy(atab[:, BC:], abase[:, :]),
                lambda: vec.memset(psA[0][:, 0:MN], 0.0),
                lambda: vec.memset(psA[1][:, 0:MN], 0.0),
            ]
            next_gather = [lambda: vec.tensor_scalar(gbase[:, :], gbase[:, :], float(W), float(NPAD), ALU.add, ALU.min)]
            next_build = [
                lambda: vec.tensor_scalar(abase[:, :], abase[:, :], float(WA), float(ND), ALU.add, ALU.min),
                lambda: vec.memset(srcq_h[:, :], -1.0),
                lambda: vec.memset(dstq_h[:, :], -1.0),
            ]
            PER0 = len(open_gather) + len(open_build) + len(next_gather) + len(next_build)

            def starts(tab, at, n, most):
                _, regs = nc.values_load_multi_w_load_instructions(
                    tab[0:1, bass.ds(at, n)], engines=[mybir.EngineType.DVE], min_val=0, max_val=most,
                    skip_runtime_bounds_check_because="the starts are clamped to it")
                return regs

            def add_gather(f, b, start, n):
                s = S[f]
                dve.wait_ge(s["added"], n + 1)
                win = acc[:, :, bass.ds(start, W)]
                vec.tensor_tensor(win, win, shares(f)[b % 2], ALU.add).then_inc(s["added"], 1)

            def add_build(b, start, n):
                dve.wait_ge(s_adda, n + 1)
                win = A[:, :, bass.ds(start, WA)]
                share = psA[b % 2][:, 0:MN].rearrange("p (q d) -> p q d", d=WA)
                vec.tensor_tensor(win, win, share, ALU.add).then_inc(s_adda, 1)

            def first_unit(u, q, qb, j, nbu):
                s = S[0]
                gst = starts(gtab, u * UB, UB, NPAD)
                ast = starts(atab, u * UB, UB, ND) if qb is not None else None
                for b in range(UB):
                    c0 = b * BC
                    dve.wait_ge(s["done"], q * UB + b + 3)
                    add_gather(0, b, gst[b], q * UB + j * BC + b)
                    if ast is not None:
                        dve.wait_ge(s_bld, qb * UB + b + 1)
                        add_build(b, ast[b], qb * UB + j * BC + b)
                    cols = bass.ds(u * UC + c0, BC)
                    for h, (tq, tr) in enumerate(((srcq_h, srcr_h), (dstq_h, dstr_h))):
                        vec.tensor_tensor(hot_r[:, h, c0:c0 + BC, :],
                                          iotr[:, :].unsqueeze(1).to_broadcast([P, BC, P]),
                                          tr[:, cols].unsqueeze(2).to_broadcast([P, BC, P]), ALU.is_equal)
                        vec.tensor_tensor(hot_q[:, h, c0:c0 + BC, :],
                                          iotr[:, 0:NT].unsqueeze(1).to_broadcast([P, BC, NT]),
                                          tq[:, cols].unsqueeze(2).to_broadcast([P, BC, NT]), ALU.is_equal)
                    for c in range(BC):
                        col = bass.ds(u * UC + c0 + c, 1)
                        if ast is not None:
                            vec.tensor_scalar(hot_m[:, c0 + c, :], iotm[:, :], key[:, col], None, ALU.is_equal)
                        last = vec.tensor_scalar(hot_w[:, c0 + c, :], iotw[:, :], dloc[:, col], wt[:, col],
                                                 ALU.is_equal, ALU.mult)
                    last.then_inc(s["hot"], 1)

            def close_build(qb, j, nbu):
                ast = starts(atab, nbu * UB, BC, ND)
                for b in range(BC):
                    dve.wait_ge(s_bld, qb * UB + b + 1)
                    add_build(b, ast[b], qb * UB + j * BC + b)

            def close_gather(f, q, j):
                gst = starts(gtab, NU * UB, BC, NPAD)
                for b in range(BC):
                    dve.wait_ge(S[f]["done"], q * UB + b + 3)
                    add_gather(f, b, gst[b], q * UB + j * BC + b)

            def first_close(q, j):
                close_gather(0, q, j)
                run_chain(S[0]["round"], j * PER0 + len(open_gather + open_build), next_gather + next_build)

            first_block_loops(
                dve, first_unit,
                ahead=lambda j: run_chain(S[0]["round"], j * PER0, open_gather + open_build),
                after_build=close_build, after=first_close)

            dve.wait_ge(s_hist, 1)
            v("ts", norm[:, :, :], hist, 1.0, None, ALU.max)
            vec.reciprocal(norm[:, :, :], norm[:, :, :]).then_inc(s_deg, 1)
            v("red", viol[:, :], hist[:, 0, :], axis=AX.X, op=ALU.max)
            vec.tensor_scalar(viol[:, :], viol[:, :], EXACT, None, ALU.is_gt).then_inc(s_viol, 1)
            dve.wait_ge(s_vsum, 1)
            v("ts", thr[:, 1:2], psH[:, P:P + 1], 0.0, None, ALU.is_equal)
            v("ts", thr[:, 0:1], thr[:, 1:2], float(ND), None, ALU.mult)
            v("ts", bt0[:, :], uidx[:, :], float(1 - NU), None, ALU.add)
            v("stt", bt1[:, :], stat[:, 1, :], thr[:, 0:1], bt0[:, :], ALU.is_ge, ALU.mult)
            v("red", scf[:, 2:3], bt1[:, :], axis=AX.X, op=ALU.min)
            v("ts", scf[:, 2:3], scf[:, 2:3], float(NU - 1), None, ALU.add)
            v("ts", scf[:, 3:4], scf[:, 2:3], -1.0, float(NU), ALU.mult, ALU.add)
            vec.tensor_copy(scal[:, 2:4], scf[:, 2:4]).then_inc(s_scal, 1)
            dve.wait_ge(s_norm, 1)

            def tail(f):
                s = S[f]
                last = f == HOPS
                normed = f == 0 or last
                for step in range(NT + 3):
                    t = step
                    if t < NT:
                        k = t % 4
                        dve.wait_ge(s["lin"], t + 1)
                        if t >= 4 and not last:
                            dve.wait_ge(s["vhi"], t - 3)
                        if t >= 4 and normed:
                            dve.wait_ge(s["out"][k], 16 * (t // 4))
                        if t < 4 and f == 1:
                            dve.wait_ge(S[0]["out"][k], 16 * len(range(k, NT, 4)))
                        if normed:
                            dve.wait_ge(s["xin"][k], 16 * (t // 4 + 1))
                        if f == 0:
                            vec.scalar_tensor_tensor(xp[:, k, :], psW[t % 2][:, 0:D], 0.0, xin[:, k, :],
                                                     ALU.max, ALU.add).then_inc(s["free"], 1)
                        elif last:
                            v("stt", xp[:, k, :], psW[t % 2][:, 0:D], norm[:, 1, t:t + 1],
                              b1s[:, f - 1, :], ALU.mult, ALU.add)
                            vec.tensor_tensor(xp[:, k, :], xp[:, k, :], xin[:, k, :],
                                              ALU.add).then_inc(s["free"], 1)
                        else:
                            vec.scalar_tensor_tensor(xp[:, k, :], psW[t % 2][:, 0:D], norm[:, 1, t:t + 1],
                                                     b1s[:, f - 1, :], ALU.mult, ALU.add).then_inc(s["nrm"], 1)
                        if normed:
                            dve.wait_ge(s["free"], t + 1)
                            v("bn", bst[:, k, :], xp[:, k, :])
                            vec.bn_aggr(mv[:, k, :], bst[:, k, :]).then_inc(s["var"], 1)
                    t = step - 1
                    if normed and 0 <= t < NT:
                        k = t % 4
                        dve.wait_ge(s["std"], t + 1)
                        v("rec", rs[:, k:k + 1], sd[:, k:k + 1])
                        vec.tensor_scalar(xp[:, k, :], xp[:, k, :], mv[:, k, 0:1], rs[:, k:k + 1],
                                          ALU.subtract, ALU.mult).then_inc(s["nrm"], 1)
                    t = step - 2
                    if not last and 0 <= t < NT:
                        k = t % 4
                        dve.wait_ge(s["vhi"], t + 1)
                        vec.tensor_tensor(vv[:, k, :], vv[:, k, :], hp[:, t, 0, :],
                                          ALU.subtract).then_inc(s["rem"], 1)
                    t = step - 3
                    if not last and 0 <= t < NT:
                        k = t % 4
                        dve.wait_ge(s["mid"], t + 1)
                        vec.tensor_tensor(hp[:, t, 2, :], vv[:, k, :], hp[:, t, 1, :],
                                          ALU.subtract).then_inc(s["low"], 1)

            ops["bn"] = nc.vector.bn_stats
            tail(0)

            select = [
                lambda: vec.tensor_tensor(per_block(dloc), per_block(dst), per_chunk(gbase), ALU.subtract),
                lambda: vec.tensor_scalar(tmp[:, :], dst[:, :], thr[:, 0:1], None, ALU.is_ge),
                lambda: vec.scalar_tensor_tensor(dsel[:, :], dloc[:, :], 1.0, tmp[:, :], ALU.add, ALU.mult),
                lambda: vec.tensor_scalar(dsel[:, :], dsel[:, :], -1.0, None, ALU.add),
                lambda: vec.tensor_copy(gtab[:, BC:], gbase[:, :]),
                lambda: vec.memset(shares(1)[0], 0.0),
                lambda: vec.memset(shares(1)[1], 0.0),
            ]
            PERH = len(select) + len(next_gather)
            for f in range(1, HOPS + 1):
                s = S[f]
                v("cp", gbase[:, :], stat[:, 0, :])

                def hop_unit(u, q, j):
                    gst = starts(gtab, u * UB, UB, NPAD)
                    for b in range(UB):
                        dve.wait_ge(s["done"], q * UB + b + 3)
                        add_gather(f, b, gst[b], q * UB + j * BC + b)
                        for c in range(BC):
                            k = b * BC + c
                            last = vec.tensor_scalar(hot_1[:, k, :], iotr[:, 0:W],
                                                     dsel[:, bass.ds(u * UC + k, 1)], None, ALU.is_equal)
                        last.then_inc(s["hot"], 1)

                def hop_close(q, j):
                    close_gather(f, q, j)
                    run_chain(s["round"], j * PERH + len(select), next_gather)

                total = hop_loops(dve, hop_unit,
                                  ahead=lambda j: run_chain(s["round"], j * PERH, select), after=hop_close)
                dve.wait_ge(s["added"], total)
                for g in range(GD):
                    dve.wait_ge(s["dense"], g + 1)
                    for h in range(HALVES):
                        dense = psD(g, h)
                        win = acc[:, h, g * GC:(g + 1) * GC]
                        vec.scalar_tensor_tensor(win, dense, thr[:, 1:2], win, ALU.mult,
                                                 ALU.add).then_inc(s["aggr"], 1)
                tail(f)

        @block.tensor
        def _(pe):
            mm = nc.tensor.matmul
            pe.wait_ge(s_const, 2)
            mm(psH[:, :], zeros[:, 0:P], zeros[:, :], start=True, stop=False)
            pe.sem_inc(s_bld, 2)
            pe.sem_inc(S[0]["done"], UB)

            def first_unit(u, q, qb, j, nbu):
                s = S[0]
                for b in range(UB):
                    slots = range(b * BC, (b + 1) * BC)
                    pe.wait_ge(s["hot"], q * UB + b + 1)
                    for k in slots:
                        for h in range(2):
                            mm(hist[:, h, :], hot_r[:, h, k, :], hot_q[:, h, k, :], start=False, stop=False)
                    if qb is not None:
                        for k in slots:
                            for a, z in ((0, GC), (GC, MN)):
                                last = mm(psA[b % 2][:, a:z], hot_r[:, 0, k, :], hot_m[:, k, a:z],
                                          start=k == slots[0], stop=k == slots[-1])
                        last.then_inc(s_bld, 1)
                    for k in slots:
                        pe.wait_ge(s["landed"][k], q * 16 + 16)
                    for h in range(HALVES):
                        for k in slots:
                            last = mm(shares(0)[b % 2][:, h, :], rows_f[:, k, h * P:(h + 1) * P], hot_w[:, k, :],
                                      start=k == slots[0], stop=k == slots[-1])
                    last.then_inc(s["done"], 1)

            first_block_loops(pe, first_unit)
            mm(psH[:, :], zeros[:, 0:P], zeros[:, :], start=False, stop=True).then_inc(s_hist, 1)
            pe.wait_ge(s_viol, 1)
            mm(psH[:, P:P + 1], ones[:, :], viol[:, :], start=True, stop=True).then_inc(s_vsum, 1)
            pe.wait_ge(s_wts, 64)
            pe.wait_ge(S[0]["added"], rounds_of(pe) * (NU * UB + BC) + 1)

            def tail(f):
                s = S[f]
                for t in range(NT):
                    if t >= 2:
                        pe.wait_ge(s["free"] if f in (0, HOPS) else s["nrm"], t - 1)
                    for h in range(HALVES):
                        lhs = acc[:, h, t * P:(t + 1) * P]
                        rhs = W1[:, f - 1, h, :] if f else W0[:, h, :]
                        last = mm(psW[t % 2][:, 0:D], lhs, rhs, start=h == 0, stop=bool(f) and h == HALVES - 1)
                    if f == 0:
                        last = mm(psW[t % 2][:, 0:D], ones[0:1, 0:P], b0s[0:1, :], start=False, stop=True)
                    last.then_inc(s["lin"], 1)

            tail(0)
            for f in range(1, HOPS + 1):
                s = S[f]
                prev = S[f - 1]
                pe.wait_ge(prev["low"], NT)
                pe.wait_ge(prev["free"] if f == 1 else prev["nrm"], NT)
                if f == 1:
                    pe.wait_ge(s_adda, rounds_of(pe) * (build_units_of(pe) * UB + BC) + 1)
                    pe.wait_ge(s_scal, 2)
                pe.sem_inc(s["done"], UB)
                units = pe.snap(rounds_of(pe) * hop_units_of(pe))

                def hop_unit(q):
                    for b in range(UB):
                        slots = range(b * BC, (b + 1) * BC)
                        pe.wait_ge(s["hot"], q * UB + b + 1)
                        for k in slots:
                            pe.wait_ge(s["landed"][k], q * 16 + 16)
                        for h in range(HALVES):
                            for k in slots:
                                for part in range(PARTS):
                                    at = part * D + h * P
                                    last = mm(shares(f)[b % 2][:, h, :], rows[:, k, at:at + P], hot_1[:, k, :],
                                              start=k == slots[0] and part == 0,
                                              stop=k == slots[-1] and part == PARTS - 1)
                        last.then_inc(s["done"], 1)

                for g in range(GD):
                    for h in range(HALVES):
                        mm(psD(g, h), zeros[:, 0:P], zeros[:, :], start=True, stop=False)
                    with pe.Fori(0, STEPS) as k:
                        for i in range(QSTEP):
                            q = k * QSTEP + i
                            for part in range(PARTS):
                                for h in range(HALVES):
                                    mm(psD(g, h), hp[:, bass.ds(q, 1), part, h * P:(h + 1) * P],
                                       A[:, bass.ds(q, 1), g * GC:(g + 1) * GC],
                                       start=False, stop=False)
                        turn = pe.snap(k + g * STEPS)
                        with pe.If(turn < units):
                            hop_unit(turn)
                    for h in range(HALVES):
                        last = mm(psD(g, h), zeros[:, 0:P], zeros[:, :], start=False, stop=True)
                    last.then_inc(s["dense"], 1)
                with pe.If(units > GD * STEPS):
                    with pe.Fori(GD * STEPS, units) as q:
                        hop_unit(q)
                pe.wait_ge(s["aggr"], GD * HALVES)
                tail(f)


def kernel(x, src, dst, edge_weight, L0_gnn_W, L0_gnn_b, L1_gnn_W, L1_gnn_b):
    import numpy as np
    import concourse.bacc as bacc
    from concourse.bass_utils import run_bass_kernel_spmd

    def padded(a, fill):
        return np.concatenate([np.asarray(a), np.full(CH * P - E, fill, np.asarray(a).dtype)])

    def columns(a):
        return np.ascontiguousarray(a.reshape(CH, P).T)

    dst_p = padded(dst, PAD_DST)
    arrays = {
        "x": np.ascontiguousarray(x),
        "src_c": columns(padded(src, 0)),
        "dst_c": columns(dst_p),
        "wt_c": columns(padded(edge_weight, 0)),
        "dst_r": np.ascontiguousarray(dst_p.reshape(NB // BC, BC * BC * P)),
        "w0": np.ascontiguousarray(L0_gnn_W),
        "b0": np.ascontiguousarray(L0_gnn_b),
        "w1": np.ascontiguousarray(L1_gnn_W),
        "b1": np.ascontiguousarray(L1_gnn_b),
    }
    nc = bacc.Bacc("TRN2", target_bir_lowering=False, num_devices=1)
    ins = [nc.dram_tensor(k + "_in", a.shape, mybir.dt.from_np(a.dtype), kind="ExternalInput").ap()
           for k, a in arrays.items()]
    out = nc.dram_tensor("out_0", (N, D), F32, kind="ExternalOutput").ap()
    gnn_program(nc, *ins, out)
    r = run_bass_kernel_spmd(nc, [{k + "_in": a for k, a in arrays.items()}], core_ids=[0])
    return r.results[0]["out_0"]
```

```python
import concourse.bass as bass
from concourse import mybir
from contextlib import ExitStack

F32 = mybir.dt.float32
F16 = mybir.dt.float16
BF16 = mybir.dt.bfloat16
I32 = mybir.dt.int32
ALU = mybir.AluOpType
ACT = mybir.ActivationFunctionType
AX = mybir.AxisListType

P = 128
N, D, E = 3125, 256, 50000
HOPS = 3
NT = -(-N // P)
NLAST = N - (NT - 1) * P
NPAD = NT * P
HALVES = D // P
PARTS = 3
BC = 2
UB = 4
UC = UB * BC
NU = -(-E // (P * UC))
CH = NU * UC
NB = NU * UB
W = 64
WA = 32
ND = 1536
GC = 512
GD = ND // GC
AW = ND + WA
ACCW = NPAD + W
MN = NT * WA
LAG = 2
QSTEP = 5
STEPS = NT // QSTEP
PAD_DST = 8000
EXACT = 256.0
EPS = 1e-5


def gnn_program(nc, x, src_c, dst_c, wt_c, dst_r, w0, b0, w1, b1, out):
    ctx = ExitStack()
    with ctx:
        def sb(name, shape, dt):
            return ctx.enter_context(nc.sbuf_tensor(name, shape, dt))

        def ps(name, shape):
            return ctx.enter_context(nc.psum_tensor(name, shape, F32))

        def sem(name):
            return ctx.enter_context(nc.semaphore(name))

        stat_d = nc.dram_tensor("stat_d", (2, NB), F32).ap()
        x1_d = nc.dram_tensor("x1_d", (NPAD, D), F32).ap()
        hp_d = nc.dram_tensor("hp_d", (N, PARTS * D), BF16).ap()

        src = sb("src", [P, CH], I32)
        dst_i = sb("dst_i", [P, CH], I32)
        dst = sb("dst", [P, CH], F32)
        dloc = sb("dloc", [P, CH], F32)
        dsel = sb("dsel", [P, CH], F32)
        key = sb("key", [P, CH], F32)
        tmp = sb("tmp", [P, CH], F32)
        srcq = sb("srcq", [P, CH], F32)
        srcq_h = sb("srcq_h", [P, CH], BF16)
        srcr_h = sb("srcr_h", [P, CH], BF16)
        srow = sb("srow", [NB // BC, 2, BC], F32)
        stat = sb("stat", [P, 2, NB], F32)
        gbase = sb("gbase", [P, NB], F32)
        wstep = sb("wstep", [P, NB], F32)
        gtab = sb("gtab", [P, BC + NB], I32)
        atab = sb("atab", [P, UB + NB], I32)
        bt0 = sb("bt0", [P, NB], F32)
        bt1 = sb("bt1", [P, NB], F32)
        bi0 = sb("bi0", [P, NB], I32)
        bi1 = sb("bi1", [P, NB], I32)
        uidx = sb("uidx", [P, NB], F32)
        scf = sb("scf", [P, 4], F32)
        scal = sb("scal", [P, 4], I32)
        thr = sb("thr", [P, 2], F32)
        iotm = sb("iotm", [P, MN], F16)
        iotr = sb("iotr", [P, P], BF16)
        iotw = sb("iotw", [P, W], F32)
        zeros = sb("zeros", [P, GC], BF16)
        ones = sb("ones", [P, P], F32)
        zcol = sb("zcol", [P, 1], F32)
        epsc = sb("epsc", [P, 1], F32)
        W0 = sb("W0", [P, HALVES, D], F32)
        W1 = sb("W1", [P, HOPS, HALVES, D], F32)
        ones_h = sb("ones_h", [P, P], BF16)
        b0s = sb("b0s", [1, D], F32)
        b0p = sb("b0p", [1, PARTS, D], BF16)
        b1s = sb("b1s", [P, HOPS, D], F32)
        A = sb("A", [P, NT, AW], BF16)
        hp = sb("hp", [P, NT, PARTS, D], BF16)
        acc = sb("acc", [P, HALVES, ACCW], F32)
        rows = sb("rows", [P, UC, PARTS * D], BF16)
        rows_f = rows[:, :, :].bitcast(F32)
        stage = sb("stage", [P, UC], I32)
        hot_1 = sb("hot_1", [P, UC, W], BF16)
        hp_flat = hp[:, :, :, :].rearrange("p q k d -> p (q k d)")
        at = [0]

        def in_hp(shape, dt):
            size = 1
            for n in shape[1:]:
                size *= n
            size *= 2 if dt in (F32, I32) else 1
            view = hp_flat[0:shape[0], at[0]:at[0] + size]
            at[0] += size
            return view if dt is BF16 else view.bitcast(dt)

        hot_m = in_hp([P, UC, MN], BF16).rearrange("p (k m) -> p k m", k=UC)
        hot_r = in_hp([P, UC, P], BF16).rearrange("p (k m) -> p k m", k=UC)
        hot_q = in_hp([P, UC, NT], BF16).rearrange("p (k m) -> p k m", k=UC)
        hot_w = in_hp([P, UC, W], F32).rearrange("p (k m) -> p k m", k=UC)
        share_a = in_hp([P, UB, MN], BF16).rearrange("p (b m) -> p b m", b=UB)
        itmp = in_hp([P, CH], I32)
        wt = in_hp([P, CH], F32)
        b0t = in_hp([1, D], F32)
        RD = BC * BC * P
        drow_i = in_hp([NB // BC, RD], I32)
        drow = in_hp([NB // BC, RD], F32)
        norm = sb("norm", [P, 2, NT], F32)
        ring = sb("ring", [P, ACCW], F32)
        indeg = ring[0:1, :]
        viol = sb("viol", [P, 1], F32)
        xin, xp, vv = (ring[:, i * 4 * D:(i + 1) * 4 * D].rearrange("p (k d) -> p k d", k=4) for i in range(3))
        bst = sb("bst", [P, 4, 6], F32)
        mv = sb("mv", [P, 4, 2], F32)
        sd = sb("sd", [P, 4], F32)
        rs = sb("rs", [P, 4], F32)

        psA = [ps(f"psA{i}", [P, 2 * GC]) for i in range(2)]
        psG = ps("psG", [P, GC])
        psH = ps("psH", [P, GC])
        psW = [ps(f"psW{i}", [P, GC]) for i in range(2)]
        hist = psH[:, 0:NT]

        def share_bank(f, i):
            return psG if i == 0 else (psH if f else psW[1])

        def share(f, b):
            at = (b % 2) * HALVES * W
            return share_bank(f, b // 2)[:, at:at + HALVES * W].rearrange("p (h d) -> p h d", h=HALVES)

        def share_deg(f, b):
            at = 2 * HALVES * W + (b % 2) * W
            return share_bank(f, b // 2)[0:1, at:at + W]

        s_in = sem("s_in")
        s_inr = sem("s_inr")
        s_wts = sem("s_wts")
        s_iota = sem("s_iota")
        s_const = sem("s_const")
        s_hist = sem("s_hist")
        s_srow = sem("s_srow")
        s_sd = sem("s_sd")
        s_st = sem("s_st")
        s_scal = sem("s_scal")
        s_dve = sem("s_dve")
        s_tick = sem("s_tick")
        s_viol = sem("s_viol")
        s_vsum = sem("s_vsum")
        s_deg = sem("s_deg")
        s_norm = sem("s_norm")
        s_bld = sem("s_bld")
        s_evac = sem("s_evac")
        s_adda = sem("s_adda")
        s_csum = sem("s_csum")
        s_ind = sem("s_ind")
        s_degs = sem("s_degs")
        s_degr = sem("s_degr")
        s_b0 = sem("s_b0")

        def phase_sems(name):
            return {
                "landed": [sem(f"{name}_landed{k}") for k in range(UC)],
                "staged": sem(f"{name}_staged"),
                "hot": sem(f"{name}_hot"),
                "done": sem(f"{name}_done"),
                "added": sem(f"{name}_added"),
                "round": sem(f"{name}_round"),
                "dense": sem(f"{name}_dense"),
                "aggr": sem(f"{name}_aggr"),
                "lin": sem(f"{name}_lin"),
                "xin": [sem(f"{name}_xin{k}") for k in range(4)],
                "free": sem(f"{name}_free"),
                "var": sem(f"{name}_var"),
                "std": sem(f"{name}_std"),
                "nrm": sem(f"{name}_nrm"),
                "vhi": sem(f"{name}_vhi"),
                "rem": sem(f"{name}_rem"),
                "mid": sem(f"{name}_mid"),
                "low": sem(f"{name}_low"),
                "out": [sem(f"{name}_out{k}") for k in range(4)],
                "hpd": sem(f"{name}_hpd"),
            }

        S = [phase_sems(f"f{k}") for k in range(HOPS + 1)]

        def tile_rows(t):
            return NLAST if t == NT - 1 else P

        def rounds_of(eng):
            return eng.value_load(scal[0:1, 0:1], min_val=1, max_val=NPAD // WA + 1)

        def build_units_of(eng):
            return eng.value_load(scal[0:1, 1:2], min_val=1, max_val=NU)

        def first_unit_of(eng):
            return eng.value_load(scal[0:1, 2:3], min_val=0, max_val=NU - 1)

        def hop_units_of(eng):
            return eng.value_load(scal[0:1, 3:4], min_val=1, max_val=NU)

        def first_block_loops(eng, unit, ahead=None, after_build=None, after=None):
            eng.wait_ge(s_scal, 1)
            rounds = rounds_of(eng)
            nbu = build_units_of(eng)
            with eng.Fori(0, rounds) as j:
                if ahead:
                    ahead(j)
                with eng.Fori(0, nbu) as u:
                    unit(u, j * NU + u, j * nbu + u, j, nbu)
                if after_build:
                    after_build(j * nbu + nbu, j, nbu)
                with eng.If(nbu < NU):
                    with eng.Fori(nbu, NU) as u:
                        unit(u, j * NU + u, None, j, nbu)
                if after:
                    after(j * NU + NU, j)

        def hop_loops(eng, unit, ahead=None, after=None):
            rounds = rounds_of(eng)
            first = first_unit_of(eng)
            units = hop_units_of(eng)
            with eng.Fori(0, rounds) as j:
                if ahead:
                    ahead(j)
                with eng.Fori(0, units) as i:
                    u = nc.s_assert_within(first + i, 0, NU - 1, skip_runtime_bounds_check_because="first + units = NU")
                    unit(u, j * units + i, j)
                if after:
                    after((j + 1) * units, j)
            return rounds * (units * UB + 2) + 1

        def col_sum(g):
            return (psA[1][0:1, 0:GC], psA[1][0:1, GC:2 * GC], psG[0:1, 0:GC])[g]

        def psD(g, h):
            return psA[g][:, h * GC:(h + 1) * GC] if g < 2 else psW[h][:, :]

        OPEN0, CLOSE0 = 14, 3
        PER0 = OPEN0 + CLOSE0

        block = ctx.enter_context(nc.Block())

        @block.sync
        def _(sp):
            sp.dma_start(drow_i[:, :], dst_r).then_inc(s_inr, 16)
            sp.dma_start(src[:, :], src_c).then_inc(s_in, 16)
            sp.dma_start(dst_i[:, :], dst_c).then_inc(s_in, 16)
            sp.dma_start(wt[:, :], wt_c).then_inc(s_in, 16)
            sp.wait_ge(s_srow, 1)
            sp.dma_start(stat_d.rearrange("k (p j) -> p k j", j=BC), srow[:, :, :]).then_inc(s_sd, 16)
            sp.wait_ge(s_sd, 16)
            sp.dma_start(stat[:, :, :], stat_d.unsqueeze(0).to_broadcast([P, 2, NB])).then_inc(s_st, 16)
            sp.dma_start(W0[:, :, :], w0.rearrange("(h p) n -> p h n", p=P)).then_inc(s_wts, 16)
            sp.dma_start(W1[:, :, :, :], w1.rearrange("k (h p) n -> p k h n", p=P)).then_inc(s_wts, 16)
            sp.dma_start(b0s[:, :], b0.unsqueeze(0)).then_inc(s_wts, 16)
            sp.dma_start(b1s[:, :, :], b1.unsqueeze(0).to_broadcast([P, HOPS, D])).then_inc(s_wts, 16)

            for f in range(HOPS + 1):
                s = S[f]
                last = f == HOPS
                source = x if f == 0 else x1_d

                def load(t):
                    k, n = t % 4, tile_rows(t)
                    if t >= 4:
                        sp.wait_ge(s["free"], t - 3)
                    if t == NT - 1 and f == 0:
                        sp.wait_ge(s_const, 2)
                    sp.dma_start(xin[0:n, k, :], source[t * P:t * P + n, :]).then_inc(s["xin"][k], 16)

                if f == 0 or last:
                    for t in range(3):
                        load(t)
                for step in range(NT + 3):
                    t, n = step, tile_rows(step)
                    if (f == 0 or last) and t < NT:
                        if t + 3 < NT:
                            load(t + 3)
                        sp.wait_ge(s["nrm"], t + 1)
                        to = x1_d[t * P:t * P + n, :] if f == 0 else out[t * P:t * P + n, :]
                        sp.dma_start(to, xp[0:n, t % 4, :]).then_inc(s["out"][t % 4], 16)
                    t, n = step - 3, tile_rows(step - 3)
                    if not last and t >= 0:
                        sp.wait_ge(s["low"], t + 1)
                        sp.dma_start(hp_d[t * P:t * P + n, :],
                                     hp[0:n, t, :, :].rearrange("p k d -> p (k d)")).then_inc(s["hpd"], 16)
                if f == 0 or last:
                    for k in range(4):
                        sp.wait_ge(s["out"][k], 16 * len(range(k, NT, 4)))
                if not last:
                    sp.wait_ge(s["hpd"], 16 * NT)

        @block.gpsimd
        def _(pool):
            pool.iota(iotm[:, :], [[1, MN]], base=0, channel_multiplier=0,
                      allow_small_or_imprecise_dtypes=True).then_inc(s_iota, 1)
            pool.iota(iotr[:, :], [[1, P]], base=0, channel_multiplier=0,
                      allow_small_or_imprecise_dtypes=True).then_inc(s_iota, 1)
            pool.iota(iotw[:, :], [[1, W]], base=0, channel_multiplier=0,
                      allow_small_or_imprecise_dtypes=True).then_inc(s_iota, 1)
            pool.iota(uidx[:, :], [[1, NU], [0, UB]], base=0, channel_multiplier=0,
                      allow_small_or_imprecise_dtypes=True).then_inc(s_iota, 1)
            pool.memset(acc[:, :, :], 0.0).then_inc(S[0]["added"], 1)

            def gather_block(s, q, b, table, buf):
                pool.wait_ge(s["staged"], q * UB + b + 1)
                pool.sem_inc(s_tick, 1)
                for c in range(BC):
                    k = b * BC + c
                    pool.indirect_dma_start(buf(k), None, table,
                                            bass.IndirectOffsetOnAxis(ap=stage[:, k:k + 1], axis=0)
                                            ).then_inc(s["landed"][k], 16)

            def first_unit(u, q, qb, j, nbu):
                for b in range(UB):
                    gather_block(S[0], q, b, x, lambda k: rows_f[:, k, 0:D])

            first_block_loops(pool, first_unit)

            for f in range(1, HOPS + 1):
                s = S[f]
                pool.wait_ge(S[f - 1]["lin"], NT)
                pool.memset(acc[:, :, :], 0.0).then_inc(s["added"], 1)
                pool.wait_ge(S[f - 1]["hpd"], 16 * NT)
                pool.wait_ge(s_scal, 2)

                def hop_unit(u, q, j):
                    for b in range(UB):
                        gather_block(s, q, b, hp_d, lambda k: rows[:, k, :])

                hop_loops(pool, hop_unit)

        @block.scalar
        def _(act):
            act.wait_ge(s_const, 1)
            nc.scalar.copy(A[:, :, :].rearrange("p q d -> p (q d)").bitcast(F32),
                           zcol[:, 0:1].to_broadcast([P, NT * AW // 2])).then_inc(s_adda, 1)
            act.sem_inc(s_adda, 2)
            act.sem_inc(s_evac, 1)
            act.wait_ge(s_in, 48)

            def stage_block(s, u, q, b):
                act.wait_ge(s["done"], q * UB + b + 1)
                nc.scalar.copy(stage[:, b * BC:(b + 1) * BC],
                               src[:, bass.ds(u * UC + b * BC, BC)]).then_inc(s["staged"], 1)

            def stage_unit(s, u, q):
                for b in range(UB):
                    stage_block(s, u, q, b)

            def evacuate(b, n, j):
                act.wait_ge(s_bld, n + 1)
                act.wait_ge(s_adda, n + 1 + j * UB)
                nc.scalar.copy(share_a[:, (b + 1) % UB, :], psA[(b + 1) % 2][:, 0:MN]).then_inc(s_evac, 1)

            def first_unit(u, q, qb, j, nbu):
                for b in range(UB):
                    stage_block(S[0], u, q, b)
                    if qb is not None:
                        evacuate(b, qb * UB + b, j)

            def close_build(qb, j, nbu):
                for b in range(UB - 1):
                    evacuate(b, qb * UB + b, j)

            def open_round(j):
                act.wait_ge(S[0]["round"], j * PER0 + OPEN0)
                act.sem_inc(s_tick, 1)

            first_block_loops(act, first_unit, ahead=open_round, after_build=close_build)

            act.wait_ge(s_deg, 1)
            nc.scalar.activation(norm[:, 0, :], norm[:, 0, :], ACT.Sqrt).then_inc(s_norm, 1)
            act.wait_ge(s_norm, 1)

            for f in range(HOPS + 1):
                s = S[f]
                last = f == HOPS
                if f > 0:
                    act.wait_ge(s_scal, 2)
                    hop_loops(act, lambda u, q, j: stage_unit(s, u, q))
                if f == 1:
                    act.wait_ge(s_deg, 2)
                    nc.scalar.activation(norm[:, 1, :], norm[:, 1, :], ACT.Sqrt).then_inc(s_norm, 1)
                for t in range(NT + 2):
                    if (f == 0 or last) and t < NT:
                        act.wait_ge(s["var"], t + 1)
                        nc.scalar.activation(sd[:, t % 4:t % 4 + 1], mv[:, t % 4, 1:2], ACT.Sqrt,
                                             bias=epsc[:, 0:1]).then_inc(s["std"], 1)
                    a = t - 1
                    if not last and 0 <= a < NT:
                        act.wait_ge(s["nrm"], a + 1)
                        if a >= 4:
                            act.wait_ge(s["low"], a - 3)
                        scale = norm[:, 0, a:a + 1]
                        nc.scalar.activation(vv[:, a % 4, :], xp[:, a % 4, :], ACT.Relu if f else ACT.Copy,
                                             scale=scale)
                        nc.scalar.activation(hp[:, a, 0, :], xp[:, a % 4, :], ACT.Relu if f else ACT.Copy,
                                             scale=scale).then_inc(s["vhi"], 1)
                    m = t - 2
                    if not last and 0 <= m < NT:
                        act.wait_ge(s["rem"], m + 1)
                        nc.scalar.copy(hp[:, m, 1, :], vv[:, m % 4, :]).then_inc(s["mid"], 1)

        @block.vector
        def _(dve):
            chain = [0]

            def link(ins):
                chain[0] += 1
                ins.then_inc(s_dve, 1)
                dve.wait_ge(s_dve, chain[0])

            ops = {"ts": nc.vector.tensor_scalar, "tt": nc.vector.tensor_tensor,
                   "stt": nc.vector.scalar_tensor_tensor, "cp": nc.vector.tensor_copy,
                   "red": nc.vector.tensor_reduce, "set": nc.vector.memset,
                   "rec": nc.vector.reciprocal}

            def v(name, *args, **kw):
                link(ops[name](*args, **kw))

            nc.vector.memset(zcol[:, :], 0.0).then_inc(s_const, 1)
            v("set", zeros[:, :], 0.0)
            v("set", ones[:, :], 1.0)
            v("set", ones_h[:, :], 1.0)
            v("set", epsc[:, :], EPS)
            v("set", gtab[:, 0:BC], 0)
            v("set", atab[:, 0:UB], 0)
            nc.vector.memset(xin[:, :, :], 0.0).then_inc(s_const, 1)
            dve.wait_ge(s_inr, 16)
            v("cp", drow[:, :], drow_i[:, :])
            rows_v = drow[:, :].rearrange("p (j e) -> p j e", j=BC)
            v("red", srow[:, 0, :], rows_v, axis=AX.X, op=ALU.min)
            v("cp", bi0[0:NB // BC, 0:BC], srow[:, 0, :])
            v("ts", bi0[0:NB // BC, 0:BC], bi0[0:NB // BC, 0:BC], -2, None, ALU.bitwise_and)
            v("cp", srow[:, 0, :], bi0[0:NB // BC, 0:BC])
            v("stt", drow[:, :], drow[:, :], float(NPAD), drow[:, :], ALU.is_lt, ALU.mult)
            nc.vector.tensor_reduce(srow[:, 1, :], rows_v, axis=AX.X, op=ALU.max).then_inc(s_srow, 1)
            dve.wait_ge(s_in, 48)
            v("cp", dst[:, :], dst_i[:, :])
            v("ts", itmp[:, :], src[:, :], P - 1, None, ALU.bitwise_and)
            v("cp", srcr_h[:, :], itmp[:, :])
            v("ts", itmp[:, :], src[:, :], 7, None, ALU.arith_shift_right)
            v("cp", srcq[:, :], itmp[:, :])
            v("ts", tmp[:, :], dst[:, :], float(NPAD), 64.0, ALU.is_ge, ALU.mult)
            v("tt", srcq_h[:, :], srcq[:, :], tmp[:, :], ALU.add)

            dve.wait_ge(s_st, 16)
            dve.wait_ge(s_iota, 4)
            v("cp", gbase[:, :], stat[:, 0, :])
            v("ts", bt0[:, :], uidx[:, :], 1.0, None, ALU.add)
            v("stt", bt1[:, :], stat[:, 0, :], float(ND), bt0[:, :], ALU.is_lt, ALU.mult)
            v("red", scf[:, 1:2], bt1[:, :], axis=AX.X, op=ALU.max)
            v("ts", scf[:, 1:2], scf[:, 1:2], 1.0, None, ALU.max)
            v("ts", wstep[:, :], uidx[:, :], scf[:, 1:2], float(WA - W), ALU.is_lt, ALU.mult)
            v("ts", wstep[:, :], wstep[:, :], float(W), None, ALU.add)
            v("tt", bt0[:, :], stat[:, 1, :], stat[:, 0, :], ALU.subtract)
            v("cp", bi0[:, :], bt0[:, :])
            v("ts", bi1[:, :], bi0[:, :], WA.bit_length() - 1, None, ALU.arith_shift_right)
            v("ts", bi0[:, :], bi0[:, :], W.bit_length() - 1, None, ALU.arith_shift_right)
            v("ts", bt0[:, :], wstep[:, :], float(WA), None, ALU.is_equal)
            v("tt", bt0[:, :], bt0[:, :], bi1[:, :], ALU.mult)
            v("tt", bt0[:, :], bt0[:, :], bi0[:, :], ALU.max)
            v("red", scf[:, 0:1], bt0[:, :], axis=AX.X, op=ALU.max)
            v("ts", scf[:, 0:1], scf[:, 0:1], 1.0, 1.0, ALU.add, ALU.max)
            nc.vector.tensor_copy(scal[:, 0:2], scf[:, 0:2]).then_inc(s_scal, 1)

            def per_chunk(tab):
                return tab[:, :].unsqueeze(2).to_broadcast([P, NB, BC])

            def per_block(tab):
                return tab[:, :].rearrange("p (b c) -> p b c", c=BC)

            def run_chain(chained, done, steps):
                for i, make in enumerate(steps):
                    make().then_inc(chained, 1)
                    dve.wait_ge(chained, done + i + 1)
                dve.sem_inc(s_tick, 1)

            vec = nc.vector
            open_first = [
                lambda: vec.tensor_tensor(per_block(dloc), per_block(dst), per_chunk(gbase), ALU.subtract),
                lambda: vec.tensor_copy(gtab[:, BC:], gbase[:, :]),
                lambda: vec.tensor_scalar(atab[:, UB:], gbase[:, :], float(ND), None, ALU.min),
                lambda: vec.memset(share_bank(0, 0)[:, :], 0.0),
                lambda: vec.memset(share_bank(0, 1)[:, :], 0.0),
                lambda: vec.memset(psA[0][:, 0:MN], 0.0),
                lambda: vec.memset(psA[1][:, 0:MN], 0.0),
                lambda: vec.memset(share_a[:, 0, :], 0.0),
                lambda: vec.scalar_tensor_tensor(key[:, :], srcq[:, :], float(WA), dloc[:, :], ALU.mult, ALU.add),
                lambda: vec.tensor_scalar(tmp[:, :], dloc[:, :], 0.0, None, ALU.is_ge),
                lambda: vec.scalar_tensor_tensor(tmp[:, :], dst[:, :], float(ND), tmp[:, :], ALU.is_lt, ALU.mult),
                lambda: vec.scalar_tensor_tensor(tmp[:, :], dloc[:, :], float(WA), tmp[:, :], ALU.is_lt, ALU.mult),
                lambda: vec.scalar_tensor_tensor(key[:, :], key[:, :], 1.0, tmp[:, :], ALU.add, ALU.mult),
                lambda: vec.tensor_scalar(key[:, :], key[:, :], -1.0, None, ALU.add),
            ]
            close_first = [
                lambda: vec.tensor_tensor(gbase[:, :], gbase[:, :], wstep[:, :], ALU.add),
                lambda: vec.tensor_scalar(gbase[:, :], gbase[:, :], float(NPAD), None, ALU.min),
                lambda: vec.memset(srcq_h[:, :], -1.0),
            ]
            assert (len(open_first), len(close_first)) == (OPEN0, CLOSE0)

            def starts(tab, at, n, most):
                _, regs = nc.values_load_multi_w_load_instructions(
                    tab[0:1, bass.ds(at, n)], engines=[mybir.EngineType.DVE], min_val=0, max_val=most,
                    skip_runtime_bounds_check_because="the starts are clamped to it")
                return regs

            def add_gather(f, b, start, n, width):
                s = S[f]
                dve.wait_ge(s["added"], n + 1)
                win = acc[:, :, bass.ds(start, width)]
                vec.tensor_tensor(win, win, share(f, b)[:, :, 0:width], ALU.add).then_inc(s["added"], 1)
                if f == 1:
                    dve.wait_ge(s_degs, n + 1)
                    win = indeg[:, bass.ds(start, width)]
                    vec.tensor_tensor(win, win, share_deg(f, b)[:, 0:width], ALU.add).then_inc(s_degs, 1)

            def add_last_pair(f, gst, q, j, width):
                dve.wait_ge(S[f]["done"], q * UB + UB)
                for i in range(2):
                    add_gather(f, 2 + i, gst[i], q * UB + j * 2 + i, width)

            def add_first_pair(f, gst, q, j, width):
                dve.wait_ge(S[f]["done"], q * UB + 2 + UB)
                for i in range(2):
                    add_gather(f, i, gst[2 + i], q * UB + j * 2 + 2 + i, width)

            def add_build(b, start, n, j):
                dve.wait_ge(s_evac, n + 1 + j * (UB - 1))
                dve.wait_ge(s_adda, n + 3 + j * UB)
                win = A[:, :, bass.ds(start, WA)]
                vec.tensor_tensor(win, win, share_a[:, b, :].rearrange("p (q d) -> p q d", d=WA),
                                  ALU.add).then_inc(s_adda, 1)

            def first_unit(u, q, qb, j, nbu):
                s = S[0]
                width = W if qb is None else WA
                for b in range(UB):
                    c0 = b * BC
                    dve.wait_ge(s["done"], q * UB + b + 1)
                    cols = bass.ds(u * UC + c0, BC)
                    vec.tensor_tensor(hot_r[:, c0:c0 + BC, :], iotr[:, :].unsqueeze(1).to_broadcast([P, BC, P]),
                                      srcr_h[:, cols].unsqueeze(2).to_broadcast([P, BC, P]), ALU.is_equal)
                    vec.tensor_tensor(hot_q[:, c0:c0 + BC, :], iotr[:, 0:NT].unsqueeze(1).to_broadcast([P, BC, NT]),
                                      srcq_h[:, cols].unsqueeze(2).to_broadcast([P, BC, NT]), ALU.is_equal)
                    for c in range(BC):
                        col = bass.ds(u * UC + c0 + c, 1)
                        if qb is not None:
                            vec.tensor_scalar(hot_m[:, c0 + c, :], iotm[:, :], key[:, col], None, ALU.is_equal)
                        last = vec.tensor_scalar(hot_w[:, c0 + c, 0:width], iotw[:, 0:width], dloc[:, col],
                                                 wt[:, col], ALU.is_equal, ALU.mult)
                    last.then_inc(s["hot"], 1)
                    if b == 0:
                        gst = starts(gtab, u * UB, UB, NPAD)
                        ast = starts(atab, u * UB, UB, ND) if qb is not None else None
                    if b == 1:
                        add_last_pair(0, gst, q, j, width)
                    if qb is not None:
                        add_build(b, ast[b], qb * UB + b, j)
                    if b == UB - 1:
                        add_first_pair(0, gst, q, j, width)

            def close_build(qb, j, nbu):
                ast = starts(atab, nbu * UB, UB, ND)
                for b in range(UB):
                    add_build(b, ast[b], qb * UB + b, j)

            def close_gather(f, q, j):
                add_last_pair(f, starts(gtab, NU * UB, 2, NPAD), q, j, W)

            def first_close(q, j):
                close_gather(0, q, j)
                run_chain(S[0]["round"], j * PER0 + OPEN0, close_first)

            dve.wait_ge(s_wts, 64)
            v("cp", b0p[:, 0, :], b0s[:, :])
            v("tt", b0t[:, :], b0s[:, :], b0p[:, 0, :], ALU.subtract)
            v("cp", b0p[:, 1, :], b0t[:, :])
            vec.tensor_tensor(b0p[:, 2, :], b0t[:, :], b0p[:, 1, :], ALU.subtract).then_inc(s_b0, 1)

            first_block_loops(dve, first_unit, ahead=lambda j: run_chain(S[0]["round"], j * PER0, open_first),
                              after_build=close_build, after=first_close)

            dve.wait_ge(s_hist, 1)
            v("ts", norm[:, 0, :], hist, 1.0, None, ALU.max)
            vec.reciprocal(norm[:, 0, :], norm[:, 0, :]).then_inc(s_deg, 1)
            v("red", viol[:, :], hist, axis=AX.X, op=ALU.max)
            vec.tensor_scalar(viol[:, :], viol[:, :], EXACT, None, ALU.is_gt).then_inc(s_viol, 1)
            dve.wait_ge(s_vsum, 1)
            v("ts", thr[:, 1:2], psH[:, P:P + 1], 0.0, None, ALU.is_equal)
            v("ts", thr[:, 0:1], thr[:, 1:2], float(ND), None, ALU.mult)
            v("ts", bt0[:, :], uidx[:, :], float(1 - NU), None, ALU.add)
            v("stt", bt1[:, :], stat[:, 1, :], thr[:, 0:1], bt0[:, :], ALU.is_ge, ALU.mult)
            v("red", scf[:, 2:3], bt1[:, :], axis=AX.X, op=ALU.min)
            v("ts", scf[:, 2:3], scf[:, 2:3], float(NU - 1), None, ALU.add)
            v("ts", scf[:, 3:4], scf[:, 2:3], -1.0, float(NU), ALU.mult, ALU.add)
            vec.tensor_copy(scal[:, 2:4], scf[:, 2:4]).then_inc(s_scal, 1)
            dve.wait_ge(s_norm, 1)

            def tail(f):
                s = S[f]
                last = f == HOPS
                normed = f == 0 or last
                for step in range(NT + 3):
                    t = step
                    if t < NT:
                        k = t % 4
                        dve.wait_ge(s["lin"], t + 1)
                        if t >= 4 and not last:
                            dve.wait_ge(s["vhi"], t - 3)
                        if t >= 4 and normed:
                            dve.wait_ge(s["out"][k], 16 * (t // 4))
                        if normed:
                            dve.wait_ge(s["xin"][k], 16 * (t // 4 + 1))
                        if f == 0:
                            vec.scalar_tensor_tensor(xp[:, k, :], psW[t % 2][:, 0:D], 0.0, xin[:, k, :],
                                                     ALU.max, ALU.add).then_inc(s["free"], 1)
                        elif last:
                            v("stt", xp[:, k, :], psW[t % 2][:, 0:D], norm[:, 1, t:t + 1],
                              b1s[:, f - 1, :], ALU.mult, ALU.add)
                            vec.tensor_tensor(xp[:, k, :], xp[:, k, :], xin[:, k, :],
                                              ALU.add).then_inc(s["free"], 1)
                        else:
                            vec.scalar_tensor_tensor(xp[:, k, :], psW[t % 2][:, 0:D], norm[:, 1, t:t + 1],
                                                     b1s[:, f - 1, :], ALU.mult, ALU.add).then_inc(s["nrm"], 1)
                        if normed:
                            dve.wait_ge(s["free"], t + 1)
                            v("bn", bst[:, k, :], xp[:, k, :])
                            vec.bn_aggr(mv[:, k, :], bst[:, k, :]).then_inc(s["var"], 1)
                    t = step - 1
                    if normed and 0 <= t < NT:
                        k = t % 4
                        dve.wait_ge(s["std"], t + 1)
                        v("rec", rs[:, k:k + 1], sd[:, k:k + 1])
                        vec.tensor_scalar(xp[:, k, :], xp[:, k, :], mv[:, k, 0:1], rs[:, k:k + 1],
                                          ALU.subtract, ALU.mult).then_inc(s["nrm"], 1)
                    t = step - 2
                    if not last and 0 <= t < NT:
                        k = t % 4
                        dve.wait_ge(s["vhi"], t + 1)
                        vec.tensor_tensor(vv[:, k, :], vv[:, k, :], hp[:, t, 0, :],
                                          ALU.subtract).then_inc(s["rem"], 1)
                    t = step - 3
                    if not last and 0 <= t < NT:
                        k = t % 4
                        dve.wait_ge(s["mid"], t + 1)
                        vec.tensor_tensor(hp[:, t, 2, :], vv[:, k, :], hp[:, t, 1, :],
                                          ALU.subtract).then_inc(s["low"], 1)

            ops["bn"] = nc.vector.bn_stats
            tail(0)

            for k in range(4):
                dve.wait_ge(S[0]["out"][k], 16 * len(range(k, NT, 4)))
            dve.wait_ge(S[0]["low"], NT)
            v("set", indeg[:, ND:], 0.0)
            for g in range(GD):
                dve.wait_ge(s_csum, g + 1)
                last = vec.tensor_scalar(indeg[:, g * GC:(g + 1) * GC], col_sum(g), thr[0:1, 1:2], None, ALU.mult)
            last.then_inc(s_ind, 1)
            dve.wait_ge(s_ind, 1)
            dve.sem_inc(s_degs, 1)

            select = [
                lambda: vec.tensor_tensor(per_block(dloc), per_block(dst), per_chunk(gbase), ALU.subtract),
                lambda: vec.tensor_scalar(tmp[:, :], dst[:, :], thr[:, 0:1], None, ALU.is_ge),
                lambda: vec.scalar_tensor_tensor(dsel[:, :], dloc[:, :], 1.0, tmp[:, :], ALU.add, ALU.mult),
                lambda: vec.tensor_scalar(dsel[:, :], dsel[:, :], -1.0, None, ALU.add),
                lambda: vec.tensor_copy(gtab[:, BC:], gbase[:, :]),
                lambda: vec.memset(share_bank(1, 0)[:, :], 0.0),
                lambda: vec.memset(share_bank(1, 1)[:, :], 0.0),
            ]
            next_gather = [
                lambda: vec.tensor_scalar(gbase[:, :], gbase[:, :], float(W), float(NPAD), ALU.add, ALU.min)]
            PERH = len(select) + len(next_gather)
            for f in range(1, HOPS + 1):
                s = S[f]
                v("cp", gbase[:, :], stat[:, 0, :])

                def hop_unit(u, q, j):
                    for b in range(UB):
                        dve.wait_ge(s["done"], q * UB + b + 1)
                        for c in range(BC):
                            k = b * BC + c
                            last = vec.tensor_scalar(hot_1[:, k, :], iotr[:, 0:W],
                                                     dsel[:, bass.ds(u * UC + k, 1)], None, ALU.is_equal)
                        last.then_inc(s["hot"], 1)
                        if b == 0:
                            gst = starts(gtab, u * UB, UB, NPAD)
                        if b == 1:
                            add_last_pair(f, gst, q, j, W)
                    add_first_pair(f, gst, q, j, W)

                def hop_close(q, j):
                    close_gather(f, q, j)
                    run_chain(s["round"], j * PERH + len(select), next_gather)

                total = hop_loops(dve, hop_unit,
                                  ahead=lambda j: run_chain(s["round"], j * PERH, select), after=hop_close)
                dve.wait_ge(s["added"], total)
                for g in range(GD):
                    dve.wait_ge(s["dense"], g + 1)
                    for h in range(HALVES):
                        dense = psD(g, h)
                        win = acc[:, h, g * GC:(g + 1) * GC]
                        vec.scalar_tensor_tensor(win, dense, thr[:, 1:2], win, ALU.mult,
                                                 ALU.add).then_inc(s["aggr"], 1)
                if f == 1:
                    dve.wait_ge(s_degs, total)
                    dve.sem_inc(s_degr, 1)
                    dve.wait_ge(s_degr, 2)
                    v("ts", norm[:, 1, :], psH[:, 0:NT], 1.0, None, ALU.max)
                    vec.reciprocal(norm[:, 1, :], norm[:, 1, :]).then_inc(s_deg, 1)
                    dve.wait_ge(s_norm, 2)
                tail(f)

        @block.tensor
        def _(pe):
            mm = nc.tensor.matmul
            pe.wait_ge(s_const, 2)
            mm(psH[:, :], zeros[:, 0:P], zeros[:, :], start=True, stop=False)
            pe.sem_inc(s_bld, 3)
            pe.sem_inc(S[0]["done"], UB)

            def first_unit(u, q, qb, j, nbu):
                s = S[0]
                for b in range(UB):
                    slots = range(b * BC, (b + 1) * BC)
                    pe.wait_ge(s["hot"], q * UB + b + 1)
                    for k in slots:
                        mm(hist, hot_r[:, k, :], hot_q[:, k, :], start=False, stop=False)
                    if qb is not None:
                        pe.wait_ge(s_evac, qb * UB + b + 3 + j * (UB - 1))
                        for k in slots:
                            for a, z in ((0, GC), (GC, MN)):
                                last = mm(psA[b % 2][:, a:z], hot_r[:, k, :], hot_m[:, k, a:z],
                                          start=k == slots[0], stop=k == slots[-1])
                        last.then_inc(s_bld, 1)
                    for k in slots:
                        pe.wait_ge(s["landed"][k], q * 16 + 16)
                    if b % 2 == 0:
                        pe.wait_ge(s["added"], q * UB + j * 2 + b + 1)
                    width = W if qb is None else WA
                    for h in range(HALVES):
                        for k in slots:
                            last = mm(share(0, b)[:, h, 0:width], rows_f[:, k, h * P:(h + 1) * P],
                                      hot_w[:, k, 0:width], start=k == slots[0], stop=k == slots[-1])
                    last.then_inc(s["done"], 1)

            first_block_loops(pe, first_unit)
            mm(psH[:, :], zeros[:, 0:P], zeros[:, :], start=False, stop=True).then_inc(s_hist, 1)
            pe.wait_ge(s_viol, 1)
            mm(psH[:, P:P + 1], ones[:, :], viol[:, :], start=True, stop=True).then_inc(s_vsum, 1)
            pe.wait_ge(s_wts, 64)
            pe.wait_ge(s_b0, 1)
            pe.wait_ge(s_scal, 1)
            pe.wait_ge(S[0]["added"], rounds_of(pe) * (NU * UB + 2) + 1)

            def tail(f):
                s = S[f]
                for t in range(NT):
                    if t >= 2:
                        pe.wait_ge(s["free"] if f in (0, HOPS) else s["nrm"], t - 1)
                    for h in range(HALVES):
                        lhs = acc[:, h, t * P:(t + 1) * P]
                        rhs = W1[:, f - 1, h, :] if f else W0[:, h, :]
                        last = mm(psW[t % 2][:, 0:D], lhs, rhs, start=h == 0, stop=bool(f) and h == HALVES - 1)
                    if f == 0:
                        for part in range(PARTS):
                            last = mm(psW[t % 2][:, 0:D], ones_h[0:1, 0:P], b0p[:, part, :], start=False,
                                      stop=part == PARTS - 1)
                    last.then_inc(s["lin"], 1)

            tail(0)
            pe.wait_ge(s_adda, rounds_of(pe) * (build_units_of(pe) * UB + UB) + 3)
            for g in range(GD):
                for q in range(NT):
                    last = mm(col_sum(g), ones_h[:, 0:1], A[:, q, g * GC:(g + 1) * GC], start=q == 0, stop=q == NT - 1)
                last.then_inc(s_csum, 1)
            for f in range(1, HOPS + 1):
                s = S[f]
                prev = S[f - 1]
                if f == 1:
                    pe.wait_ge(s_scal, 2)
                pe.sem_inc(s["done"], UB)
                units = pe.snap(rounds_of(pe) * hop_units_of(pe))

                def hop_unit(q):
                    for b in range(UB):
                        slots = range(b * BC, (b + 1) * BC)
                        pe.wait_ge(s["hot"], q * UB + b + 1)
                        for k in slots:
                            pe.wait_ge(s["landed"][k], q * 16 + 16)
                        if b % 2 == 0:
                            pe.wait_ge(s["added"], q * UB + b + 1)
                        if f == 1:
                            for k in slots:
                                mm(share_deg(f, b), ones_h[:, 0:1], hot_1[:, k, :],
                                   start=k == slots[0], stop=k == slots[-1])
                        for h in range(HALVES):
                            for k in slots:
                                for part in range(PARTS):
                                    at = part * D + h * P
                                    last = mm(share(f, b)[:, h, :], rows[:, k, at:at + P], hot_1[:, k, :],
                                              start=k == slots[0] and part == 0,
                                              stop=k == slots[-1] and part == PARTS - 1)
                        last.then_inc(s["done"], 1)

                def dense_step(g, k):
                    if g == 0:
                        pe.wait_ge(prev["low"], k * QSTEP + QSTEP)
                    for i in range(QSTEP):
                        q = k * QSTEP + i
                        for part in range(PARTS):
                            for h in range(HALVES):
                                mm(psD(g, h), hp[:, bass.ds(q, 1), part, h * P:(h + 1) * P],
                                   A[:, bass.ds(q, 1), g * GC:(g + 1) * GC], start=False, stop=False)

                def dense_and_unit(g, k, q):
                    dense_step(g, k)
                    with pe.If(q < units):
                        hop_unit(q)

                for g in range(GD):
                    if g == 1 and f == 1:
                        pe.wait_ge(s_ind, 1)
                    if g == GD - 1:
                        pe.wait_ge(prev["free"] if f == 1 else prev["nrm"], NT)
                    for h in range(HALVES):
                        mm(psD(g, h), zeros[:, 0:P], zeros[:, :], start=True, stop=False)
                    if g == 0:
                        with pe.Fori(0, LAG) as k:
                            dense_step(g, k)
                        with pe.Fori(0, STEPS - LAG) as q:
                            dense_and_unit(g, q + LAG, q)
                    else:
                        with pe.Fori(0, STEPS) as k:
                            dense_and_unit(g, k, pe.snap(k + (g * STEPS - LAG)))
                    for h in range(HALVES):
                        last = mm(psD(g, h), zeros[:, 0:P], zeros[:, :], start=False, stop=True)
                    last.then_inc(s["dense"], 1)
                with pe.If(units > GD * STEPS - LAG):
                    with pe.Fori(GD * STEPS - LAG, units) as q:
                        hop_unit(q)
                if f == 1:
                    pe.wait_ge(s_degr, 1)
                    for t in range(NT):
                        last = mm(psH[:, t:t + 1], indeg[:, t * P:(t + 1) * P], ones[0:1, 0:1], start=True, stop=True)
                    last.then_inc(s_degr, 1)
                pe.wait_ge(s["aggr"], GD * HALVES)
                tail(f)


def kernel(x, src, dst, edge_weight, L0_gnn_W, L0_gnn_b, L1_gnn_W, L1_gnn_b):
    import numpy as np
    import concourse.bacc as bacc
    from concourse.bass_utils import run_bass_kernel_spmd

    def padded(a, fill):
        return np.concatenate([np.asarray(a), np.full(CH * P - E, fill, np.asarray(a).dtype)])

    def columns(a):
        return np.ascontiguousarray(a.reshape(CH, P).T)

    dst_p = padded(dst, PAD_DST)
    arrays = {
        "x": np.ascontiguousarray(x),
        "src_c": columns(padded(src, 0)),
        "dst_c": columns(dst_p),
        "wt_c": columns(padded(edge_weight, 0)),
        "dst_r": np.ascontiguousarray(dst_p.reshape(NB // BC, BC * BC * P)),
        "w0": np.ascontiguousarray(L0_gnn_W),
        "b0": np.ascontiguousarray(L0_gnn_b),
        "w1": np.ascontiguousarray(L1_gnn_W),
        "b1": np.ascontiguousarray(L1_gnn_b),
    }
    nc = bacc.Bacc("TRN2", target_bir_lowering=False, num_devices=1)
    ins = [nc.dram_tensor(k + "_in", a.shape, mybir.dt.from_np(a.dtype), kind="ExternalInput").ap()
           for k, a in arrays.items()]
    out = nc.dram_tensor("out_0", (N, D), F32, kind="ExternalOutput").ap()
    gnn_program(nc, *ins, out)
    r = run_bass_kernel_spmd(nc, [{k + "_in": a for k, a in arrays.items()}], core_ids=[0])
    return r.results[0]["out_0"]
```

```python
import concourse.bass as bass
from concourse import mybir
from contextlib import ExitStack

F32 = mybir.dt.float32
F16 = mybir.dt.float16
BF16 = mybir.dt.bfloat16
I32 = mybir.dt.int32
ALU = mybir.AluOpType
ACT = mybir.ActivationFunctionType
AX = mybir.AxisListType

P = 128
N, D, E = 3125, 256, 50000
HOPS = 3
NT = -(-N // P)
NLAST = N - (NT - 1) * P
NPAD = NT * P
HALVES = D // P
PARTS = 3
BC = 2
UB = 4
UC = UB * BC
NU = -(-E // (P * UC))
CH = NU * UC
NB = NU * UB
W = 64
WB = 32
WA = 16
ND = 1536
GC = 512
GD = ND // GC
AW = ND + WA
ACCW = NPAD + W
MN = NT * WA
LAG = 2
QSTEP = 5
STEPS = NT // QSTEP
PAD_DST = 8000
EXACT = 256.0
EPS = 1e-5


def gnn_program(nc, x, src_c, dst_c, wt_c, dst_r, w0, b0, w1, b1, out):
    ctx = ExitStack()
    with ctx:
        def sb(name, shape, dt):
            return ctx.enter_context(nc.sbuf_tensor(name, shape, dt))

        def ps(name, shape):
            return ctx.enter_context(nc.psum_tensor(name, shape, F32))

        def sem(name):
            return ctx.enter_context(nc.semaphore(name))

        stat_d = nc.dram_tensor("stat_d", (2, CH), F32).ap()
        x1_d = nc.dram_tensor("x1_d", (NPAD, D), F32).ap()
        deg_d = nc.dram_tensor("deg_d", (NPAD,), F32).ap()
        hp_d = nc.dram_tensor("hp_d", (N, PARTS * D), BF16).ap()

        src = sb("src", [P, CH], I32)
        dst_i = sb("dst_i", [P, CH], I32)
        dst = sb("dst", [P, CH], F32)
        dloc = sb("dloc", [P, CH], F32)
        dsel = sb("dsel", [P, CH], F32)
        tmp = sb("tmp", [P, CH], F32)
        edge_tab = sb("edge_tab", [P, NU, 5, UC], F32)
        unit_tab = sb("unit_tab", [P, 5, UC], F32)
        KEY, SRCR, LOC, WT, SRCT = range(5)
        srow = sb("srow", [NB // BC, 2, BC * BC], F32)
        stat = sb("stat", [P, 2, CH], F32)
        gbase = sb("gbase", [P, NB], F32)
        gtab = sb("gtab", [P, BC + NB], I32)
        uidx = sb("uidx", [P, NB], F32)
        scf = sb("scf", [P, 4], F32)
        scal = sb("scal", [P, 4], I32)
        thr = sb("thr", [P, 2], F32)
        iotm = sb("iotm", [P, MN], F16)
        iotr = sb("iotr", [P, P], BF16)
        iotw = sb("iotw", [P, W], F32)
        zeros = sb("zeros", [P, GC], BF16)
        ones = sb("ones", [P, P], F32)
        zcol = sb("zcol", [P, 1], F32)
        epsc = sb("epsc", [P, 1], F32)
        W0 = sb("W0", [P, HALVES, D], F32)
        W1 = sb("W1", [P, HOPS, HALVES, D], F32)
        ones_h = sb("ones_h", [P, P], BF16)
        b0s = sb("b0s", [1, D], F32)
        b0p = sb("b0p", [1, PARTS, D], BF16)
        b1s = sb("b1s", [P, HOPS, D], F32)
        A = sb("A", [P, NT, AW], BF16)
        hp = sb("hp", [P, NT, PARTS, D], BF16)
        acc = sb("acc", [P, HALVES, ACCW], F32)
        rows = sb("rows", [P, UC, PARTS * D], BF16)
        rows_f = rows[:, :, :].bitcast(F32)
        stage = sb("stage", [P, UC], I32)
        hot_1 = sb("hot_1", [P, UC, W], BF16)
        hp_flat = hp[:, :, :, :].rearrange("p q k d -> p (q k d)")
        at = [0]

        def in_hp(shape, dt):
            size = 1
            for n in shape[1:]:
                size *= n
            size *= 2 if dt in (F32, I32) else 1
            view = hp_flat[0:shape[0], at[0]:at[0] + size]
            at[0] += size
            return view if dt is BF16 else view.bitcast(dt)

        hot_m = in_hp([P, UC, MN], BF16).rearrange("p (k m) -> p k m", k=UC)
        hot_r = in_hp([P, UC, P], BF16).rearrange("p (k m) -> p k m", k=UC)
        hot_q = in_hp([P, UC, NT], BF16).rearrange("p (k m) -> p k m", k=UC)
        hot_w = in_hp([P, UC, W], F32).rearrange("p (k m) -> p k m", k=UC)
        share_a = in_hp([P, UC, MN], BF16).rearrange("p (k m) -> p k m", k=UC)
        itmp = in_hp([P, CH], I32)
        wt = in_hp([P, CH], F32)
        srcq = in_hp([P, CH], F32)
        cbase = in_hp([P, CH], F32)
        cloc = in_hp([P, CH], F32)
        atab = in_hp([P, UC + CH], I32)
        wstep = in_hp([P, NB], F32)
        bt0 = in_hp([P, NB], F32)
        bt1 = in_hp([P, NB], F32)
        RD = BC * BC * P
        drow_i = in_hp([NB // BC, RD], I32)
        drow = in_hp([NB // BC, RD], F32)
        norm = sb("norm", [P, 2, NT], F32)
        ring = sb("ring", [P, ACCW], F32)
        indeg = ring[0:1, :]
        viol = sb("viol", [P, 1], F32)
        xp = ring[:, 0:4 * D].rearrange("p (k d) -> p k d", k=4)
        vv = ring[:, 4 * D:8 * D].rearrange("p (k d) -> p k d", k=4)
        xin = ring[:, 8 * D:12 * D].rearrange("p (k d) -> p k d", k=4)
        res = ring[:, 4 * D:12 * D].rearrange("p (k d) -> p k d", k=8)
        bst = sb("bst", [P, 4, 6], F32)
        mv = sb("mv", [P, 4, 2], F32)
        sd = sb("sd", [P, 4], F32)
        rs = sb("rs", [P, 4], F32)

        psA = [ps(f"psA{i}", [P, 2 * GC]) for i in range(2)]
        psG = ps("psG", [P, GC])
        psH = ps("psH", [P, GC])
        psW = [ps(f"psW{i}", [P, GC]) for i in range(2)]
        hist = psH[:, 0:NT]

        def share_bank(f, i):
            return psG if i == 0 else (psH if f else psW[1])

        def share(f, b):
            at = (b % 2) * HALVES * W
            return share_bank(f, b // 2)[:, at:at + HALVES * W].rearrange("p (h d) -> p h d", h=HALVES)

        def share_deg(f, b):
            at = 2 * HALVES * W + (b % 2) * W
            return share_bank(f, b // 2)[0:1, at:at + W]

        s_in = sem("s_in")
        s_inr = sem("s_inr")
        s_wts = sem("s_wts")
        s_iota = sem("s_iota")
        s_const = sem("s_const")
        s_hist = sem("s_hist")
        s_srow = sem("s_srow")
        s_sd = sem("s_sd")
        s_st = sem("s_st")
        s_scal = sem("s_scal")
        s_dve = sem("s_dve")
        s_tick = sem("s_tick")
        s_viol = sem("s_viol")
        s_vsum = sem("s_vsum")
        s_deg = sem("s_deg")
        s_norm = sem("s_norm")
        s_bld = sem("s_bld")
        s_clear = sem("s_clear")
        s_eq = sem("s_eq")
        s_unit = sem("s_unit")
        s_res = sem("s_res")
        s_evac = sem("s_evac")
        s_adda = sem("s_adda")
        s_csum = sem("s_csum")
        s_ind = sem("s_ind")
        s_degs = sem("s_degs")
        s_degr = sem("s_degr")
        s_degd = sem("s_degd")
        s_turn = sem("s_turn")
        s_b0 = sem("s_b0")

        def phase_sems(name, normed):
            return {
                "landed": [sem(f"{name}_landed{k}") for k in range(UC)],
                "staged": sem(f"{name}_staged"),
                "hot": sem(f"{name}_hot"),
                "done": sem(f"{name}_done"),
                "added": sem(f"{name}_added"),
                "round": sem(f"{name}_round"),
                "dense": sem(f"{name}_dense"),
                "aggr": sem(f"{name}_aggr"),
                "lin": sem(f"{name}_lin"),
                "xin": [sem(f"{name}_xin{k}") for k in range(8 if name == f"f{HOPS}" else 4)] if normed else None,
                "free": sem(f"{name}_free"),
                "var": sem(f"{name}_var"),
                "std": sem(f"{name}_std"),
                "nrm": sem(f"{name}_nrm"),
                "vhi": sem(f"{name}_vhi"),
                "rem": sem(f"{name}_rem"),
                "mid": sem(f"{name}_mid"),
                "low": sem(f"{name}_low"),
                "out": [sem(f"{name}_out{k}") for k in range(4)] if normed else None,
                "hpd": sem(f"{name}_hpd"),
            }

        S = [phase_sems(f"f{k}", k in (0, HOPS)) for k in range(HOPS + 1)]

        def tile_rows(t):
            return NLAST if t == NT - 1 else P

        def rounds_of(eng):
            return eng.value_load(scal[0:1, 0:1], min_val=1, max_val=NPAD // WA + 1)

        def build_units_of(eng):
            return eng.value_load(scal[0:1, 1:2], min_val=1, max_val=NU)

        def first_unit_of(eng):
            return eng.value_load(scal[0:1, 2:3], min_val=0, max_val=NU - 1)

        def hop_units_of(eng):
            return eng.value_load(scal[0:1, 3:4], min_val=1, max_val=NU)

        def first_block_loops(eng, unit, ahead=None, after_build=None, after=None):
            eng.wait_ge(s_scal, 1)
            rounds = rounds_of(eng)
            nbu = build_units_of(eng)
            with eng.Fori(0, rounds) as j:
                if ahead:
                    ahead(j)
                with eng.Fori(0, nbu) as u:
                    unit(u, j * NU + u, j * nbu + u, j, nbu)
                if after_build:
                    after_build(j * nbu + nbu, j, nbu)
                with eng.If(nbu < NU):
                    with eng.Fori(nbu, NU) as u:
                        unit(u, j * NU + u, None, j, nbu)
                if after:
                    after(j * NU + NU, j)

        def hop_loops(eng, unit, ahead=None, after=None):
            rounds = rounds_of(eng)
            first = first_unit_of(eng)
            units = hop_units_of(eng)
            with eng.Fori(0, rounds) as j:
                if ahead:
                    ahead(j)
                with eng.Fori(0, units) as i:
                    u = nc.s_assert_within(first + i, 0, NU - 1, skip_runtime_bounds_check_because="first + units = NU")
                    unit(u, j * units + i, j)
                if after:
                    after((j + 1) * units, j)
            return rounds * (units * UB + 2) + 1

        def build_bank(b):
            return psA[b % 2][:, :].rearrange("p (c m) -> p c m", c=BC)[:, :, 0:MN]

        def col_sum(g):
            return (psA[1][0:1, 0:GC], psA[1][0:1, GC:2 * GC], psG[0:1, 0:GC])[g]

        def psD(g, h):
            return psA[g][:, h * GC:(h + 1) * GC] if g < 2 else psW[h][:, :]

        OPEN0, CLOSE0 = 11, 4
        PER0 = OPEN0 + CLOSE0
        ADDA = 1 + 2 * BC

        block = ctx.enter_context(nc.Block())

        @block.sync
        def _(sp):
            sp.dma_start(drow_i[:, :], dst_r).then_inc(s_inr, 16)
            sp.dma_start(src[:, :], src_c).then_inc(s_in, 16)
            sp.dma_start(dst_i[:, :], dst_c).then_inc(s_in, 16)
            sp.dma_start(wt[:, :], wt_c).then_inc(s_in, 16)
            sp.wait_ge(s_srow, 1)
            sp.dma_start(stat_d.rearrange("k (p j) -> p k j", j=BC * BC), srow[:, :, :]).then_inc(s_sd, 16)
            sp.wait_ge(s_sd, 16)
            sp.dma_start(stat[:, :, :], stat_d.unsqueeze(0).to_broadcast([P, 2, CH])).then_inc(s_st, 16)
            sp.dma_start(W0[:, :, :], w0.rearrange("(h p) n -> p h n", p=P)).then_inc(s_wts, 16)
            sp.dma_start(W1[:, :, :, :], w1.rearrange("k (h p) n -> p k h n", p=P)).then_inc(s_wts, 16)
            sp.dma_start(b0s[:, :], b0.unsqueeze(0)).then_inc(s_wts, 16)
            sp.dma_start(b1s[:, :, :], b1.unsqueeze(0).to_broadcast([P, HOPS, D])).then_inc(s_wts, 16)

            for f in range(HOPS + 1):
                s = S[f]
                last = f == HOPS
                source = x if f == 0 else x1_d

                slots = res if last else xin
                depth = slots.shape[1]

                def load(t):
                    k, n = t % depth, tile_rows(t)
                    if t >= depth:
                        sp.wait_ge(s["free"], t - depth + 1)
                    if t == NT - 1 and f == 0:
                        sp.wait_ge(s_const, 2)
                    sp.dma_start(slots[0:n, k, :], source[t * P:t * P + n, :]).then_inc(s["xin"][k], 16)

                if f == 0 or last:
                    for t in range(depth - 1):
                        load(t)
                if f == 1:
                    sp.wait_ge(s_degr, 1)
                    sp.dma_start(deg_d.unsqueeze(0), indeg[:, 0:NPAD]).then_inc(s_degd, 16)
                    sp.wait_ge(s_degd, 16)
                    with nc.allow_non_contiguous_dma(reason="one node per partition"):
                        sp.dma_start(norm[:, 1, :], deg_d.rearrange("(t p) -> p t", p=P)).then_inc(s_turn, 16)
                for step in range(NT + 3):
                    t, n = step, tile_rows(step)
                    if (f == 0 or last) and t < NT:
                        if t + depth - 1 < NT:
                            load(t + depth - 1)
                        sp.wait_ge(s["nrm"], t + 1)
                        to = x1_d[t * P:t * P + n, :] if f == 0 else out[t * P:t * P + n, :]
                        sp.dma_start(to, xp[0:n, t % 4, :]).then_inc(s["out"][t % 4], 16)
                    t, n = step - 3, tile_rows(step - 3)
                    if not last and t >= 0:
                        sp.wait_ge(s["low"], t + 1)
                        sp.dma_start(hp_d[t * P:t * P + n, :],
                                     hp[0:n, t, :, :].rearrange("p k d -> p (k d)")).then_inc(s["hpd"], 16)
                if f == 0 or last:
                    for k in range(4):
                        sp.wait_ge(s["out"][k], 16 * len(range(k, NT, 4)))
                if not last:
                    sp.wait_ge(s["hpd"], 16 * NT)

        @block.gpsimd
        def _(pool):
            pool.iota(iotm[:, :], [[1, MN]], base=0, channel_multiplier=0,
                      allow_small_or_imprecise_dtypes=True).then_inc(s_iota, 1)
            pool.iota(iotr[:, :], [[1, P]], base=0, channel_multiplier=0,
                      allow_small_or_imprecise_dtypes=True).then_inc(s_iota, 1)
            pool.iota(iotw[:, :], [[1, W]], base=0, channel_multiplier=0,
                      allow_small_or_imprecise_dtypes=True).then_inc(s_iota, 1)
            pool.iota(uidx[:, :], [[1, NU], [0, UB]], base=0, channel_multiplier=0,
                      allow_small_or_imprecise_dtypes=True).then_inc(s_iota, 1)
            pool.memset(acc[:, :, :], 0.0).then_inc(S[0]["added"], 1)

            pool.wait_ge(s_wts, 64)
            rest = vv[0:1, 0, :]
            nc.gpsimd.tensor_copy(b0p[:, 0, :], b0s[:, :]).then_inc(s_b0, 1)
            pool.wait_ge(s_b0, 1)
            nc.gpsimd.tensor_tensor(rest, b0s[:, :], b0p[:, 0, :], ALU.subtract).then_inc(s_b0, 1)
            pool.wait_ge(s_b0, 2)
            nc.gpsimd.tensor_copy(b0p[:, 1, :], rest).then_inc(s_b0, 1)
            pool.wait_ge(s_b0, 3)
            nc.gpsimd.tensor_tensor(b0p[:, 2, :], rest, b0p[:, 1, :], ALU.subtract).then_inc(s_b0, 1)

            def gather_block(s, q, b, table, buf):
                pool.wait_ge(s["staged"], q * UB + b + 1)
                pool.sem_inc(s_tick, 1)
                for c in range(BC):
                    k = b * BC + c
                    pool.indirect_dma_start(buf(k), None, table,
                                            bass.IndirectOffsetOnAxis(ap=stage[:, k:k + 1], axis=0)
                                            ).then_inc(s["landed"][k], 16)

            def first_unit(u, q, qb, j, nbu):
                for b in range(UB):
                    gather_block(S[0], q, b, x, lambda k: rows_f[:, k, 0:D])

            first_block_loops(pool, first_unit)

            for f in range(1, HOPS + 1):
                s = S[f]
                pool.wait_ge(S[f - 1]["lin"], NT)
                pool.memset(acc[:, :, :], 0.0).then_inc(s["added"], 1)
                pool.wait_ge(S[f - 1]["hpd"], 16 * NT)
                pool.wait_ge(s_scal, 2)

                def hop_unit(u, q, j):
                    for b in range(UB):
                        gather_block(s, q, b, hp_d, lambda k: rows[:, k, :])

                hop_loops(pool, hop_unit)
            s = S[HOPS]
            for t in range(NT):
                k = t % 8
                pool.wait_ge(s["xin"][k], 16 * (t // 8 + 1))
                nc.gpsimd.tensor_tensor(res[:, k, :], res[:, k, :], b1s[:, HOPS - 1, :],
                                        ALU.add).then_inc(s_res, 1)

        @block.scalar
        def _(act):
            act.wait_ge(s_const, 1)
            nc.scalar.copy(A[:, :, :].rearrange("p q d -> p (q d)").bitcast(F32),
                           zcol[:, 0:1].to_broadcast([P, NT * AW // 2])).then_inc(s_adda, 1)
            act.sem_inc(s_adda, ADDA - 1)
            act.sem_inc(s_evac, 1)
            act.wait_ge(s_in, 48)

            def stage_block(s, u, q, b):
                act.wait_ge(s["done"], q * UB + b + 1)
                nc.scalar.copy(stage[:, b * BC:(b + 1) * BC],
                               src[:, bass.ds(u * UC + b * BC, BC)]).then_inc(s["staged"], 1)

            def stage_unit(s, u, q):
                for b in range(UB):
                    stage_block(s, u, q, b)

            def evacuate(b, n, j):
                act.wait_ge(s_bld, n + 1)
                act.wait_ge(s_adda, (n + j * UB) * BC + 1)
                slot = (b + 1) % UB * BC
                nc.scalar.copy(share_a[:, slot:slot + BC, :], build_bank(b + 1)).then_inc(s_evac, 1)

            def first_unit(u, q, qb, j, nbu):
                for b in range(UB):
                    stage_block(S[0], u, q, b)
                    if qb is not None:
                        evacuate(b, qb * UB + b, j)

            def close_build(qb, j, nbu):
                for b in range(UB - 1):
                    evacuate(b, qb * UB + b, j)

            def clear():
                for view in (share_bank(0, 0)[:, :], share_bank(0, 1)[:, :], build_bank(0), build_bank(1),
                             share_a[:, 0:BC, :]):
                    zero = zcol[:, 0:1]
                    for n in view.shape[2:]:
                        zero = zero.unsqueeze(2)
                    nc.scalar.copy(view, zero.to_broadcast(list(view.shape))).then_inc(s_clear, 1)

            def open_round(j):
                with act.If(j > 0):
                    act.wait_ge(S[0]["round"], j * PER0 + 1)
                    act.sem_inc(s_tick, 1)
                    clear()
                act.wait_ge(s_clear, j * 5 + 5)
                act.sem_inc(s_tick, 1)

            act.wait_ge(s_const, 1)
            clear()
            first_block_loops(act, first_unit, ahead=open_round, after_build=close_build)

            act.wait_ge(s_deg, 1)
            nc.scalar.activation(norm[:, 0, :], norm[:, 0, :], ACT.Sqrt).then_inc(s_norm, 1)
            act.wait_ge(s_norm, 1)

            for f in range(HOPS + 1):
                s = S[f]
                last = f == HOPS
                if f > 0:
                    act.wait_ge(s_scal, 2)
                    hop_loops(act, lambda u, q, j: stage_unit(s, u, q))
                if f == 1:
                    act.wait_ge(s_deg, 2)
                    nc.scalar.activation(norm[:, 1, :], norm[:, 1, :], ACT.Sqrt).then_inc(s_norm, 1)
                for t in range(NT + 2):
                    if (f == 0 or last) and t < NT:
                        act.wait_ge(s["var"], t + 1)
                        nc.scalar.activation(sd[:, t % 4:t % 4 + 1], mv[:, t % 4, 1:2], ACT.Sqrt,
                                             bias=epsc[:, 0:1]).then_inc(s["std"], 1)
                    a = t - 1
                    if not last and 0 <= a < NT:
                        act.wait_ge(s["nrm"], a + 1)
                        if a >= 4:
                            act.wait_ge(s["low"], a - 3)
                        scale = norm[:, 0, a:a + 1]
                        nc.scalar.activation(vv[:, a % 4, :], xp[:, a % 4, :], ACT.Relu if f else ACT.Copy,
                                             scale=scale)
                        nc.scalar.activation(hp[:, a, 0, :], xp[:, a % 4, :], ACT.Relu if f else ACT.Copy,
                                             scale=scale).then_inc(s["vhi"], 1)
                    m = t - 2
                    if not last and 0 <= m < NT:
                        act.wait_ge(s["rem"], m + 1)
                        nc.scalar.copy(hp[:, m, 1, :], vv[:, m % 4, :]).then_inc(s["mid"], 1)

        @block.vector
        def _(dve):
            chain = [0]

            def start(ins):
                chain[0] += 1
                ins.then_inc(s_dve, 1)
                return chain[0]

            def link(ins):
                dve.wait_ge(s_dve, start(ins))

            ops = {"ts": nc.vector.tensor_scalar, "tt": nc.vector.tensor_tensor,
                   "stt": nc.vector.scalar_tensor_tensor, "cp": nc.vector.tensor_copy,
                   "red": nc.vector.tensor_reduce, "set": nc.vector.memset,
                   "rec": nc.vector.reciprocal}

            def v(name, *args, **kw):
                link(ops[name](*args, **kw))

            def by_unit(tab):
                return tab[:, :].rearrange("p (u c) -> p u c", c=UC)

            def column(i):
                return edge_tab[:, :, i, :]

            def per_chunk(tab):
                return tab[:, :].unsqueeze(2).to_broadcast([P, NB, BC])

            def per_block(tab):
                return tab[:, :].rearrange("p (b c) -> p b c", c=BC)

            nc.vector.memset(zcol[:, :], 0.0).then_inc(s_const, 1)
            v("set", zeros[:, :], 0.0)
            v("set", ones[:, :], 1.0)
            v("set", ones_h[:, :], 1.0)
            v("set", epsc[:, :], EPS)
            v("set", gtab[:, 0:BC], 0)
            v("set", atab[:, 0:UC], 0)
            nc.vector.memset(xin[:, :, :], 0.0).then_inc(s_const, 1)
            dve.wait_ge(s_inr, 16)
            v("cp", drow[:, :], drow_i[:, :])
            rows_v = drow[:, :].rearrange("p (j e) -> p j e", j=BC * BC)
            v("red", srow[:, 0, :], rows_v, axis=AX.X, op=ALU.min)
            even = itmp[0:NB // BC, 0:BC * BC]
            v("cp", even, srow[:, 0, :])
            v("ts", even, even, -2, None, ALU.bitwise_and)
            v("cp", srow[:, 0, :], even)
            v("stt", drow[:, :], drow[:, :], float(NPAD), drow[:, :], ALU.is_lt, ALU.mult)
            nc.vector.tensor_reduce(srow[:, 1, :], rows_v, axis=AX.X, op=ALU.max).then_inc(s_srow, 1)
            dve.wait_ge(s_in, 48)
            v("cp", dst[:, :], dst_i[:, :])
            v("ts", itmp[:, :], src[:, :], P - 1, None, ALU.bitwise_and)
            v("cp", column(SRCR), by_unit(itmp))
            v("cp", column(WT), by_unit(wt))
            v("ts", itmp[:, :], src[:, :], 7, None, ALU.arith_shift_right)
            v("cp", srcq[:, :], itmp[:, :])
            v("ts", tmp[:, :], dst[:, :], float(NPAD), 64.0, ALU.is_ge, ALU.mult)
            v("tt", column(SRCT), by_unit(srcq), by_unit(tmp), ALU.add)

            dve.wait_ge(s_st, 16)
            dve.wait_ge(s_iota, 4)
            v("red", gbase[:, :], per_block(stat[:, 0, :]), axis=AX.X, op=ALU.min)
            v("cp", cbase[:, :], stat[:, 0, :])
            v("ts", bt0[:, :], uidx[:, :], 1.0, None, ALU.add)
            v("stt", bt1[:, :], gbase[:, :], float(ND), bt0[:, :], ALU.is_lt, ALU.mult)
            v("red", scf[:, 1:2], bt1[:, :], axis=AX.X, op=ALU.max)
            v("ts", scf[:, 1:2], scf[:, 1:2], 1.0, None, ALU.max)
            v("ts", wstep[:, :], uidx[:, :], scf[:, 1:2], float(WB - W), ALU.is_lt, ALU.mult)
            v("ts", wstep[:, :], wstep[:, :], float(W), None, ALU.add)
            v("tt", tmp[:, :], stat[:, 1, :], stat[:, 0, :], ALU.subtract)
            v("red", bt0[:, :], per_block(tmp), axis=AX.X, op=ALU.max)
            v("ts", bt0[:, :], bt0[:, :], 1.0 / WA, None, ALU.mult)
            v("stt", bt0[:, :], wstep[:, :], float(WB), bt0[:, :], ALU.is_equal, ALU.mult)
            v("red", bt1[:, :], per_block(stat[:, 1, :]), axis=AX.X, op=ALU.max)
            v("tt", bt1[:, :], bt1[:, :], gbase[:, :], ALU.subtract)
            v("ts", tmp[:, 0:NB], wstep[:, :], float(WB), float(W // WB - 1), ALU.is_equal, ALU.mult)
            v("ts", tmp[:, 0:NB], tmp[:, 0:NB], 1.0, 1.0 / W, ALU.add, ALU.mult)
            v("tt", bt1[:, :], bt1[:, :], tmp[:, 0:NB], ALU.mult)
            v("tt", bt0[:, :], bt0[:, :], bt1[:, :], ALU.max)
            v("red", scf[:, 0:1], bt0[:, :], axis=AX.X, op=ALU.max)
            v("ts", scal[:, 0:1], scf[:, 0:1], float(W), None, ALU.mult)
            v("ts", scal[:, 0:1], scal[:, 0:1], W.bit_length() - 1, None, ALU.arith_shift_right)
            v("cp", scf[:, 0:1], scal[:, 0:1])
            v("ts", scf[:, 0:1], scf[:, 0:1], 1.0, 1.0, ALU.add, ALU.max)
            nc.vector.tensor_copy(scal[:, 0:2], scf[:, 0:2]).then_inc(s_scal, 1)

            def open_block(j):
                run_chain(S[0]["round"], j * PER0, open_first)
                dve.wait_ge(s_clear, j * 5 + 5)
                dve.sem_inc(s_tick, 1)

            def run_chain(chained, done, steps):
                for i, make in enumerate(steps):
                    make().then_inc(chained, 1)
                    dve.wait_ge(chained, done + i + 1)
                dve.sem_inc(s_tick, 1)

            vec = nc.vector
            open_first = [
                lambda: vec.tensor_tensor(per_block(dloc), per_block(dst), per_chunk(gbase), ALU.subtract),
                lambda: vec.tensor_copy(column(LOC), by_unit(dloc)),
                lambda: vec.tensor_copy(gtab[:, BC:], gbase[:, :]),
                lambda: vec.tensor_tensor(cloc[:, :], dst[:, :], cbase[:, :], ALU.subtract),
                lambda: vec.tensor_scalar(atab[:, UC:], cbase[:, :], float(ND), None, ALU.min),
                lambda: vec.scalar_tensor_tensor(column(KEY), by_unit(srcq), float(WA), by_unit(cloc),
                                                 ALU.mult, ALU.add),
                lambda: vec.tensor_scalar(tmp[:, :], cloc[:, :], 0.0, None, ALU.is_ge),
                lambda: vec.scalar_tensor_tensor(tmp[:, :], dst[:, :], float(ND), tmp[:, :], ALU.is_lt, ALU.mult),
                lambda: vec.scalar_tensor_tensor(tmp[:, :], cloc[:, :], float(WA), tmp[:, :], ALU.is_lt, ALU.mult),
                lambda: vec.scalar_tensor_tensor(column(KEY), column(KEY), 1.0, by_unit(tmp), ALU.add, ALU.mult),
                lambda: vec.tensor_scalar(column(KEY), column(KEY), -1.0, None, ALU.add),
            ]
            close_first = [
                lambda: vec.tensor_tensor(gbase[:, :], gbase[:, :], wstep[:, :], ALU.add),
                lambda: vec.tensor_scalar(gbase[:, :], gbase[:, :], float(NPAD), None, ALU.min),
                lambda: vec.tensor_scalar(cbase[:, :], cbase[:, :], float(WA), float(NPAD), ALU.add, ALU.min),
                lambda: vec.memset(column(SRCT), -1.0),
            ]
            assert (len(open_first), len(close_first)) == (OPEN0, CLOSE0)

            def starts(tab, at, n, most):
                _, regs = nc.values_load_multi_w_load_instructions(
                    tab[0:1, bass.ds(at, n)], engines=[mybir.EngineType.DVE], min_val=0, max_val=most,
                    skip_runtime_bounds_check_because="the starts are clamped to it")
                return regs

            def add_gather(f, b, start, n, width):
                s = S[f]
                dve.wait_ge(s["added"], n + 1)
                win = acc[:, :, bass.ds(start, width)]
                vec.tensor_tensor(win, win, share(f, b)[:, :, 0:width], ALU.add).then_inc(s["added"], 1)
                if f == 1:
                    dve.wait_ge(s_degs, n + 1)
                    win = indeg[:, bass.ds(start, width)]
                    vec.tensor_tensor(win, win, share_deg(f, b)[:, 0:width], ALU.add).then_inc(s_degs, 1)

            def add_last_pair(f, gst, q, j, width, between=lambda i: None):
                dve.wait_ge(S[f]["done"], q * UB + UB)
                for i in range(2):
                    add_gather(f, 2 + i, gst[i], q * UB + j * 2 + i, width)
                    between(i)

            def add_first_pair(f, gst, q, j, width, between=lambda i: None):
                dve.wait_ge(S[f]["done"], q * UB + 2 + UB)
                for i in range(2):
                    add_gather(f, i, gst[2 + i], q * UB + j * 2 + 2 + i, width)
                    between(i)

            def add_build(b, c, starts, n, j):
                if c == 0:
                    dve.wait_ge(s_evac, n + 1 + j * (UB - 1))
                dve.wait_ge(s_adda, (n + j * UB) * BC + c + ADDA)
                win = A[:, :, bass.ds(starts[b * BC + c], WA)]
                vec.tensor_tensor(win, win, share_a[:, b * BC + c, :].rearrange("p (q d) -> p q d", d=WA),
                                  ALU.add).then_inc(s_adda, 1)

            def first_unit(u, q, qb, j, nbu):
                s = S[0]
                width = W if qb is None else WB
                vec.tensor_copy(unit_tab[:, :, :].rearrange("p i c -> p (i c)"),
                                edge_tab[:, :, :, :].rearrange("p u i c -> p (u i c)")[:, bass.ds(u * 5 * UC, 5 * UC)]
                                ).then_inc(s_unit, 1)
                gst = starts(gtab, u * UB, UB, NPAD)
                ast = starts(atab, u * UC, UC, ND) if qb is not None else None
                dve.wait_ge(s_unit, q + 1)

                def build_add(b, c):
                    if qb is not None:
                        add_build(b, c, ast, qb * UB + b, j)

                for b in range(UB):
                    c0 = b * BC
                    dve.wait_ge(s["done"], q * UB + b + 1)
                    hot = hot_w[:, c0:c0 + BC, 0:width]

                    def spread(i, n):
                        return unit_tab[:, i, c0:c0 + BC].unsqueeze(2).to_broadcast([P, BC, n])

                    vec.tensor_tensor(hot, iotw[:, 0:width].unsqueeze(1).to_broadcast([P, BC, width]),
                                      spread(LOC, width), ALU.is_equal).then_inc(s_eq, 1)
                    if b >= 2:
                        build_add(b - 1, 0)
                    vec.tensor_tensor(hot_q[:, c0:c0 + BC, :], iotr[:, 0:NT].unsqueeze(1).to_broadcast([P, BC, NT]),
                                      spread(SRCT, NT), ALU.is_equal)
                    for c in range(BC):
                        k = c0 + c
                        last = vec.tensor_scalar(hot_r[:, k, :], iotr[:, :], unit_tab[:, SRCR, k:k + 1], None, ALU.is_equal)
                        if qb is not None:
                            last = vec.tensor_scalar(hot_m[:, k, :], iotm[:, :], unit_tab[:, KEY, k:k + 1], None,
                                                     ALU.is_equal)
                        if c == 0:
                            dve.wait_ge(s_eq, q * UB + b + 1)
                            vec.tensor_tensor(hot, hot, spread(WT, width), ALU.mult)
                            if b >= 2:
                                build_add(b - 1, 1)
                    last.then_inc(s["hot"], 1)
                    if b == 1:
                        add_last_pair(0, gst, q, j, width, lambda i: build_add(0, i))
                add_first_pair(0, gst, q, j, width, lambda i: build_add(UB - 1, i))

            def close_build(qb, j, nbu):
                ast = starts(atab, nbu * UC, UC, ND)
                for b in range(UB):
                    for c in range(BC):
                        add_build(b, c, ast, qb * UB + b, j)

            def close_gather(f, q, j):
                add_last_pair(f, starts(gtab, NU * UB, 2, NPAD), q, j, W)

            def first_close(q, j):
                close_gather(0, q, j)
                run_chain(S[0]["round"], j * PER0 + OPEN0, close_first)

            first_block_loops(dve, first_unit, ahead=open_block,
                              after_build=close_build, after=first_close)

            dve.wait_ge(s_hist, 1)
            v("ts", norm[:, 0, :], hist, 1.0, None, ALU.max)
            vec.reciprocal(norm[:, 0, :], norm[:, 0, :]).then_inc(s_deg, 1)
            v("red", viol[:, :], hist, axis=AX.X, op=ALU.max)
            vec.tensor_scalar(viol[:, :], viol[:, :], EXACT, None, ALU.is_gt).then_inc(s_viol, 1)
            dve.wait_ge(s_vsum, 1)
            v("ts", thr[:, 1:2], psH[:, P:P + 1], 0.0, None, ALU.is_equal)
            v("ts", thr[:, 0:1], thr[:, 1:2], float(ND), None, ALU.mult)
            v("ts", bt0[:, :], uidx[:, :], float(1 - NU), None, ALU.add)
            v("red", bt1[:, :], per_block(stat[:, 1, :]), axis=AX.X, op=ALU.max)
            v("stt", bt1[:, :], bt1[:, :], thr[:, 0:1], bt0[:, :], ALU.is_ge, ALU.mult)
            v("red", scf[:, 2:3], bt1[:, :], axis=AX.X, op=ALU.min)
            v("ts", scf[:, 2:3], scf[:, 2:3], float(NU - 1), None, ALU.add)
            v("ts", scf[:, 3:4], scf[:, 2:3], -1.0, float(NU), ALU.mult, ALU.add)
            vec.tensor_copy(scal[:, 2:4], scf[:, 2:4]).then_inc(s_scal, 1)
            dve.wait_ge(s_norm, 1)

            def tail(f):
                s = S[f]
                last = f == HOPS
                normed = f == 0 or last
                for step in range(NT + 3):
                    t = step
                    if t < NT:
                        k = t % 4
                        dve.wait_ge(s["lin"], t + 1)
                        if t >= 4 and not last:
                            dve.wait_ge(s["vhi"], t - 3)
                        if t >= 4 and normed:
                            dve.wait_ge(s["out"][k], 16 * (t // 4))
                        if f == 0:
                            dve.wait_ge(s["xin"][k], 16 * (t // 4 + 1))
                        if last:
                            dve.wait_ge(s_res, t + 1)
                        if f == 0:
                            vec.scalar_tensor_tensor(xp[:, k, :], psW[t % 2][:, 0:D], 0.0, xin[:, k, :],
                                                     ALU.max, ALU.add).then_inc(s["free"], 1)
                        elif last:
                            vec.scalar_tensor_tensor(xp[:, k, :], psW[t % 2][:, 0:D], norm[:, 1, t:t + 1],
                                                     res[:, t % 8, :], ALU.mult, ALU.add).then_inc(s["free"], 1)
                        else:
                            vec.scalar_tensor_tensor(xp[:, k, :], psW[t % 2][:, 0:D], norm[:, 1, t:t + 1],
                                                     b1s[:, f - 1, :], ALU.mult, ALU.add).then_inc(s["nrm"], 1)
                    k, kb = t % 4, (t - 1) % 4
                    before = normed and 1 <= t < NT + 1
                    if before:
                        dve.wait_ge(s["std"], t)
                        inverse = start(vec.reciprocal(rs[:, kb:kb + 1], sd[:, kb:kb + 1]))
                    if normed and t < NT:
                        dve.wait_ge(s["free"], t + 1)
                        stats = start(vec.bn_stats(bst[:, k, :], xp[:, k, :]))
                    if before:
                        dve.wait_ge(s_dve, inverse)
                        vec.tensor_scalar(xp[:, kb, :], xp[:, kb, :], mv[:, kb, 0:1], rs[:, kb:kb + 1],
                                          ALU.subtract, ALU.mult).then_inc(s["nrm"], 1)
                    if normed and t < NT:
                        dve.wait_ge(s_dve, stats)
                        vec.bn_aggr(mv[:, k, :], bst[:, k, :]).then_inc(s["var"], 1)
                    t = step - 2
                    if not last and 0 <= t < NT:
                        k = t % 4
                        dve.wait_ge(s["vhi"], t + 1)
                        vec.tensor_tensor(vv[:, k, :], vv[:, k, :], hp[:, t, 0, :],
                                          ALU.subtract).then_inc(s["rem"], 1)
                    t = step - 3
                    if not last and 0 <= t < NT:
                        k = t % 4
                        dve.wait_ge(s["mid"], t + 1)
                        vec.tensor_tensor(hp[:, t, 2, :], vv[:, k, :], hp[:, t, 1, :],
                                          ALU.subtract).then_inc(s["low"], 1)

            tail(0)

            for k in range(4):
                dve.wait_ge(S[0]["out"][k], 16 * len(range(k, NT, 4)))
            dve.wait_ge(S[0]["low"], NT)
            v("set", indeg[:, ND:], 0.0)
            dve.wait_ge(s_csum, 1)
            for g in range(GD):
                last = vec.tensor_scalar(indeg[:, g * GC:(g + 1) * GC], col_sum(g), thr[0:1, 1:2], None, ALU.mult)
            last.then_inc(s_ind, 1)
            dve.wait_ge(s_ind, 1)
            dve.sem_inc(s_degs, 1)

            select = [
                lambda: vec.tensor_tensor(per_block(dloc), per_block(dst), per_chunk(gbase), ALU.subtract),
                lambda: vec.tensor_scalar(tmp[:, :], dst[:, :], thr[:, 0:1], None, ALU.is_ge),
                lambda: vec.scalar_tensor_tensor(dsel[:, :], dloc[:, :], 1.0, tmp[:, :], ALU.add, ALU.mult),
                lambda: vec.tensor_scalar(dsel[:, :], dsel[:, :], -1.0, None, ALU.add),
                lambda: vec.tensor_copy(gtab[:, BC:], gbase[:, :]),
                lambda: vec.memset(share_bank(1, 0)[:, :], 0.0),
                lambda: vec.memset(share_bank(1, 1)[:, :], 0.0),
            ]
            next_gather = [
                lambda: vec.tensor_scalar(gbase[:, :], gbase[:, :], float(W), float(NPAD), ALU.add, ALU.min)]
            PERH = len(select) + len(next_gather)
            for f in range(1, HOPS + 1):
                s = S[f]
                v("red", gbase[:, :], per_block(stat[:, 0, :]), axis=AX.X, op=ALU.min)

                def hop_unit(u, q, j):
                    for b in range(UB):
                        dve.wait_ge(s["done"], q * UB + b + 1)
                        for c in range(BC):
                            k = b * BC + c
                            last = vec.tensor_scalar(hot_1[:, k, :], iotr[:, 0:W],
                                                     dsel[:, bass.ds(u * UC + k, 1)], None, ALU.is_equal)
                        last.then_inc(s["hot"], 1)
                        if b == 0:
                            gst = starts(gtab, u * UB, UB, NPAD)
                        if b == 1:
                            add_last_pair(f, gst, q, j, W)
                    add_first_pair(f, gst, q, j, W)

                def hop_close(q, j):
                    close_gather(f, q, j)
                    run_chain(s["round"], j * PERH + len(select), next_gather)

                total = hop_loops(dve, hop_unit,
                                  ahead=lambda j: run_chain(s["round"], j * PERH, select), after=hop_close)
                dve.wait_ge(s["added"], total)
                if f == 1:
                    dve.wait_ge(s_degs, total)
                    dve.sem_inc(s_degr, 1)
                dve.wait_ge(s["dense"], GD)
                for g in (GD - 1, *range(GD - 1)):
                    for h in range(HALVES):
                        dense = psD(g, h)
                        win = acc[:, h, g * GC:(g + 1) * GC]
                        vec.scalar_tensor_tensor(win, dense, thr[:, 1:2], win, ALU.mult,
                                                 ALU.add).then_inc(s["aggr"], 1)
                if f == 1:
                    dve.wait_ge(s_turn, 16)
                    v("ts", norm[:, 1, :], norm[:, 1, :], 1.0, None, ALU.max)
                    vec.reciprocal(norm[:, 1, :], norm[:, 1, :]).then_inc(s_deg, 1)
                    dve.wait_ge(s_norm, 2)
                tail(f)

        @block.tensor
        def _(pe):
            mm = nc.tensor.matmul
            pe.wait_ge(s_const, 2)
            mm(psH[:, :], zeros[:, 0:P], zeros[:, :], start=True, stop=False)
            pe.sem_inc(s_bld, 3)
            pe.sem_inc(S[0]["done"], UB)

            def first_unit(u, q, qb, j, nbu):
                s = S[0]
                for b in range(UB):
                    slots = range(b * BC, (b + 1) * BC)
                    pe.wait_ge(s["hot"], q * UB + b + 1)
                    for k in slots:
                        mm(hist, hot_r[:, k, :], hot_q[:, k, :], start=False, stop=False)
                    if qb is not None:
                        pe.wait_ge(s_evac, qb * UB + b + 3 + j * (UB - 1))
                        for k in slots:
                            last = mm(psA[b % 2][:, (k - slots[0]) * GC:(k - slots[0]) * GC + MN], hot_r[:, k, :],
                                      hot_m[:, k, :], start=True, stop=True)
                        last.then_inc(s_bld, 1)
                    for k in slots:
                        pe.wait_ge(s["landed"][k], q * 16 + 16)
                    if b % 2 == 0:
                        pe.wait_ge(s["added"], q * UB + j * 2 + b + 1)
                    width = W if qb is None else WB
                    for h in range(HALVES):
                        for k in slots:
                            last = mm(share(0, b)[:, h, 0:width], rows_f[:, k, h * P:(h + 1) * P],
                                      hot_w[:, k, 0:width], start=k == slots[0], stop=k == slots[-1])
                    last.then_inc(s["done"], 1)

            first_block_loops(pe, first_unit)
            mm(psH[:, :], zeros[:, 0:P], zeros[:, :], start=False, stop=True).then_inc(s_hist, 1)
            pe.wait_ge(s_wts, 64)
            pe.wait_ge(s_b0, 4)
            pe.wait_ge(s_scal, 1)
            rounds, build_units = rounds_of(pe), build_units_of(pe)
            pe.wait_ge(S[0]["added"], rounds * (NU * UB + 2) + 1)

            def tail(f):
                s = S[f]
                for t in range(NT):
                    if t >= 2:
                        pe.wait_ge(s["free"] if f in (0, HOPS) else s["nrm"], t - 1)
                    if f and t * P % GC == 0 and t * P // GC < GD - 1:
                        pe.wait_ge(s["aggr"], (t * P // GC + 2) * HALVES)
                    for h in range(HALVES):
                        lhs = acc[:, h, t * P:(t + 1) * P]
                        rhs = W1[:, f - 1, h, :] if f else W0[:, h, :]
                        last = mm(psW[t % 2][:, 0:D], lhs, rhs, start=h == 0, stop=bool(f) and h == HALVES - 1)
                    if f == 0:
                        for part in range(PARTS):
                            last = mm(psW[t % 2][:, 0:D], ones_h[0:1, 0:P], b0p[:, part, :], start=False,
                                      stop=part == PARTS - 1)
                    last.then_inc(s["lin"], 1)
                    if f == 0:
                        for g in range(GD):
                            last = mm(col_sum(g), ones_h[:, 0:1], A[:, t, g * GC:(g + 1) * GC],
                                      start=t == 0, stop=t == NT - 1)
                        if t == NT - 1:
                            last.then_inc(s_csum, 1)
                        if t == 0:
                            pe.wait_ge(s_viol, 1)
                            mm(psH[:, P:P + 1], ones[:, :], viol[:, :], start=True, stop=True).then_inc(s_vsum, 1)

            pe.wait_ge(s_adda, rounds * (build_units * UC + UC) + ADDA)
            tail(0)
            for f in range(1, HOPS + 1):
                s = S[f]
                prev = S[f - 1]
                if f == 1:
                    pe.wait_ge(s_scal, 2)
                pe.sem_inc(s["done"], UB)
                units = pe.snap(rounds_of(pe) * hop_units_of(pe))

                def hop_unit(q, before=lambda b: None):
                    for b in range(UB):
                        before(b)
                        slots = range(b * BC, (b + 1) * BC)
                        pe.wait_ge(s["hot"], q * UB + b + 1)
                        for k in slots:
                            pe.wait_ge(s["landed"][k], q * 16 + 16)
                        if b % 2 == 0:
                            pe.wait_ge(s["added"], q * UB + b + 1)
                        if f == 1:
                            for k in slots:
                                mm(share_deg(f, b), ones_h[:, 0:1], hot_1[:, k, :],
                                   start=k == slots[0], stop=k == slots[-1])
                        for h in range(HALVES):
                            for k in slots:
                                for part in range(PARTS):
                                    at = part * D + h * P
                                    last = mm(share(f, b)[:, h, :], rows[:, k, at:at + P], hot_1[:, k, :],
                                              start=k == slots[0] and part == 0,
                                              stop=k == slots[-1] and part == PARTS - 1)
                        last.then_inc(s["done"], 1)

                def dense_tile(g, k, i):
                    q = k * QSTEP + i
                    if g == 0:
                        pe.wait_ge(prev["low"], q + 1)
                    for part in range(PARTS):
                        for h in range(HALVES):
                            mm(psD(g, h), hp[:, bass.ds(q, 1), part, h * P:(h + 1) * P],
                               A[:, bass.ds(q, 1), g * GC:(g + 1) * GC], start=False, stop=False)

                def dense_step(g, k):
                    for i in range(QSTEP):
                        dense_tile(g, k, i)

                def dense_and_unit(g, k, q):
                    with pe.If(q < units):
                        hop_unit(q, before=lambda b: dense_tile(g, k, b))
                        for i in range(UB, QSTEP):
                            dense_tile(g, k, i)
                    with pe.If(q >= units):
                        dense_step(g, k)

                for g in range(GD):
                    if g == 1 and f == 1:
                        pe.wait_ge(s_ind, 1)
                    if g == GD - 1:
                        pe.wait_ge(prev["free"] if f == 1 else prev["nrm"], NT)
                    for h in range(HALVES):
                        mm(psD(g, h), zeros[:, 0:P], zeros[:, :], start=True, stop=False)
                    if g == 0:
                        with pe.Fori(0, LAG) as k:
                            dense_step(g, k)
                        with pe.Fori(0, STEPS - LAG) as q:
                            dense_and_unit(g, q + LAG, q)
                    else:
                        with pe.Fori(0, STEPS) as k:
                            dense_and_unit(g, k, pe.snap(k + (g * STEPS - LAG)))
                    for h in range(HALVES):
                        last = mm(psD(g, h), zeros[:, 0:P], zeros[:, :], start=False, stop=True)
                    last.then_inc(s["dense"], 1)
                with pe.If(units > GD * STEPS - LAG):
                    with pe.Fori(GD * STEPS - LAG, units) as q:
                        hop_unit(q)
                tail(f)


def kernel(x, src, dst, edge_weight, L0_gnn_W, L0_gnn_b, L1_gnn_W, L1_gnn_b):
    import numpy as np
    import concourse.bacc as bacc
    from concourse.bass_utils import run_bass_kernel_spmd

    def padded(a, fill):
        return np.concatenate([np.asarray(a), np.full(CH * P - E, fill, np.asarray(a).dtype)])

    def columns(a):
        return np.ascontiguousarray(a.reshape(CH, P).T)

    dst_p = padded(dst, PAD_DST)
    arrays = {
        "x": np.ascontiguousarray(x),
        "src_c": columns(padded(src, 0)),
        "dst_c": columns(dst_p),
        "wt_c": columns(padded(edge_weight, 0)),
        "dst_r": np.ascontiguousarray(dst_p.reshape(NB // BC, BC * BC * P)),
        "w0": np.ascontiguousarray(L0_gnn_W),
        "b0": np.ascontiguousarray(L0_gnn_b),
        "w1": np.ascontiguousarray(L1_gnn_W),
        "b1": np.ascontiguousarray(L1_gnn_b),
    }
    nc = bacc.Bacc("TRN2", target_bir_lowering=False, num_devices=1)
    ins = [nc.dram_tensor(k + "_in", a.shape, mybir.dt.from_np(a.dtype), kind="ExternalInput").ap()
           for k, a in arrays.items()]
    out = nc.dram_tensor("out_0", (N, D), F32, kind="ExternalOutput").ap()
    gnn_program(nc, *ins, out)
    r = run_bass_kernel_spmd(nc, [{k + "_in": a for k, a in arrays.items()}], core_ids=[0])
    return r.results[0]["out_0"]
```
